# Optimizing a Trainium2 kernel written in Bass

```python
import numpy as np
import jax
import jax.numpy as jnp

def _softmax(x, axis=-1):
    return jax.nn.softmax(x, axis=axis)

def _gelu(x):
    return jax.nn.gelu(x, approximate=True)

def _silu(x):
    return jax.nn.silu(x)

def _sigmoid(x):
    return jax.nn.sigmoid(x)

def _layernorm(x, axis=-1, eps=1e-05):
    m = jnp.mean(x, axis=axis, keepdims=True)
    v = jnp.var(x, axis=axis, keepdims=True)
    return (x - m) / jnp.sqrt(v + eps)

def _scatter_add(tgt, idx, src, axis=0):
    return tgt.at[idx].add(src)

def _segment_sum(src, seg, n):
    return jax.ops.segment_sum(src, seg, n)
kernel_name = 'mk_dlrm_tower_d1_rec_r8_45c507'

def setup_inputs(seed: int=0):
    np.random.seed(seed)
    _w = jnp.asarray

    def _rec_inputs():
        import jax
        import jax.numpy as jnp
        _tk = jax.random.key(seed)
        ids = jnp.stack([jax.random.randint(jax.random.fold_in(_tk, 200 + f), (2048,), 0, v, jnp.int32) for f, v in enumerate([1250, 1000, 12500, 125000, 1000, 12500, 1000, 1000, 1250, 12500, 1000, 1000, 1000, 1000, 12500, 1000, 12500, 1250, 12500, 1000, 12500, 12500, 12500, 1250, 1000, 1000])], axis=1)
        tbl_0 = 0.05 * jax.random.normal(jax.random.fold_in(_tk, 500 + 0), (1250, 128), jnp.float32)
        tbl_1 = 0.05 * jax.random.normal(jax.random.fold_in(_tk, 500 + 1), (1000, 128), jnp.float32)
        tbl_2 = 0.05 * jax.random.normal(jax.random.fold_in(_tk, 500 + 2), (12500, 128), jnp.float32)
        tbl_3 = 0.05 * jax.random.normal(jax.random.fold_in(_tk, 500 + 3), (125000, 128), jnp.float32)
        tbl_4 = 0.05 * jax.random.normal(jax.random.fold_in(_tk, 500 + 4), (1000, 128), jnp.float32)
        tbl_5 = 0.05 * jax.random.normal(jax.random.fold_in(_tk, 500 + 5), (12500, 128), jnp.float32)
        tbl_6 = 0.05 * jax.random.normal(jax.random.fold_in(_tk, 500 + 6), (1000, 128), jnp.float32)
        tbl_7 = 0.05 * jax.random.normal(jax.random.fold_in(_tk, 500 + 7), (1000, 128), jnp.float32)
        tbl_8 = 0.05 * jax.random.normal(jax.random.fold_in(_tk, 500 + 8), (1250, 128), jnp.float32)
        tbl_9 = 0.05 * jax.random.normal(jax.random.fold_in(_tk, 500 + 9), (12500, 128), jnp.float32)
        tbl_10 = 0.05 * jax.random.normal(jax.random.fold_in(_tk, 500 + 10), (1000, 128), jnp.float32)
        tbl_11 = 0.05 * jax.random.normal(jax.random.fold_in(_tk, 500 + 11), (1000, 128), jnp.float32)
        tbl_12 = 0.05 * jax.random.normal(jax.random.fold_in(_tk, 500 + 12), (1000, 128), jnp.float32)
        tbl_13 = 0.05 * jax.random.normal(jax.random.fold_in(_tk, 500 + 13), (1000, 128), jnp.float32)
        tbl_14 = 0.05 * jax.random.normal(jax.random.fold_in(_tk, 500 + 14), (12500, 128), jnp.float32)
        tbl_15 = 0.05 * jax.random.normal(jax.random.fold_in(_tk, 500 + 15), (1000, 128), jnp.float32)
        tbl_16 = 0.05 * jax.random.normal(jax.random.fold_in(_tk, 500 + 16), (12500, 128), jnp.float32)
        tbl_17 = 0.05 * jax.random.normal(jax.random.fold_in(_tk, 500 + 17), (1250, 128), jnp.float32)
        tbl_18 = 0.05 * jax.random.normal(jax.random.fold_in(_tk, 500 + 18), (12500, 128), jnp.float32)
        tbl_19 = 0.05 * jax.random.normal(jax.random.fold_in(_tk, 500 + 19), (1000, 128), jnp.float32)
        tbl_20 = 0.05 * jax.random.normal(jax.random.fold_in(_tk, 500 + 20), (12500, 128), jnp.float32)
        tbl_21 = 0.05 * jax.random.normal(jax.random.fold_in(_tk, 500 + 21), (12500, 128), jnp.float32)
        tbl_22 = 0.05 * jax.random.normal(jax.random.fold_in(_tk, 500 + 22), (12500, 128), jnp.float32)
        tbl_23 = 0.05 * jax.random.normal(jax.random.fold_in(_tk, 500 + 23), (1250, 128), jnp.float32)
        tbl_24 = 0.05 * jax.random.normal(jax.random.fold_in(_tk, 500 + 24), (1000, 128), jnp.float32)
        tbl_25 = 0.05 * jax.random.normal(jax.random.fold_in(_tk, 500 + 25), (1000, 128), jnp.float32)
        _rk = jax.random.fold_in(_tk, 7)
        r_dense_features = -0.000520686 + 1.00062 * jax.random.normal(jax.random.fold_in(_rk, 101), (2048, 128), jnp.float32)
        W_top1 = 0.0405887 * jax.random.normal(jax.random.fold_in(_tk, 801), (607, 512), jnp.float32)
        W_top2 = 0.0441942 * jax.random.normal(jax.random.fold_in(_tk, 802), (512, 256), jnp.float32)
        W_top3 = 0.0625 * jax.random.normal(jax.random.fold_in(_tk, 803), (256, 1), jnp.float32)
        b_top1 = jnp.zeros((512,), jnp.float32)
        b_top2 = jnp.zeros((256,), jnp.float32)
        return (r_dense_features, ids, tbl_0, tbl_1, tbl_2, tbl_3, tbl_4, tbl_5, tbl_6, tbl_7, tbl_8, tbl_9, tbl_10, tbl_11, tbl_12, tbl_13, tbl_14, tbl_15, tbl_16, tbl_17, tbl_18, tbl_19, tbl_20, tbl_21, tbl_22, tbl_23, tbl_24, tbl_25, W_top1, b_top1, W_top2, b_top2, W_top3)
    r_dense_features, ids, tbl_0, tbl_1, tbl_2, tbl_3, tbl_4, tbl_5, tbl_6, tbl_7, tbl_8, tbl_9, tbl_10, tbl_11, tbl_12, tbl_13, tbl_14, tbl_15, tbl_16, tbl_17, tbl_18, tbl_19, tbl_20, tbl_21, tbl_22, tbl_23, tbl_24, tbl_25, W_top1, b_top1, W_top2, b_top2, W_top3 = _rec_inputs()

    def _L0_rec_setup():
        import jax, jax.numpy as jnp
        import numpy as np
        NUM_SPARSE = 26
        EMBED_DIM = 128
        BATCH = 2048
        key = jax.random.key(seed)
        k1, k2 = jax.random.split(key)
        dense_features = jax.random.normal(k1, (BATCH, EMBED_DIM), dtype=jnp.float32)
        sparse_features = jax.random.normal(k2, (BATCH, NUM_SPARSE, EMBED_DIM), dtype=jnp.float32)
        return {'dense_features': dense_features, 'sparse_features': sparse_features}
    _L0_rec_all = _L0_rec_setup()
    _L0_rec_in = {k: v for k, v in _L0_rec_all.items() if k in ()}
    del _L0_rec_all
    return {'r_dense_features': r_dense_features, 'ids': ids, 'tbl_0': tbl_0, 'tbl_1': tbl_1, 'tbl_2': tbl_2, 'tbl_3': tbl_3, 'tbl_4': tbl_4, 'tbl_5': tbl_5, 'tbl_6': tbl_6, 'tbl_7': tbl_7, 'tbl_8': tbl_8, 'tbl_9': tbl_9, 'tbl_10': tbl_10, 'tbl_11': tbl_11, 'tbl_12': tbl_12, 'tbl_13': tbl_13, 'tbl_14': tbl_14, 'tbl_15': tbl_15, 'tbl_16': tbl_16, 'tbl_17': tbl_17, 'tbl_18': tbl_18, 'tbl_19': tbl_19, 'tbl_20': tbl_20, 'tbl_21': tbl_21, 'tbl_22': tbl_22, 'tbl_23': tbl_23, 'tbl_24': tbl_24, 'tbl_25': tbl_25, 'W_top1': W_top1, 'b_top1': b_top1, 'W_top2': W_top2, 'b_top2': b_top2, 'W_top3': W_top3}

def reference(r_dense_features, ids, tbl_0, tbl_1, tbl_2, tbl_3, tbl_4, tbl_5, tbl_6, tbl_7, tbl_8, tbl_9, tbl_10, tbl_11, tbl_12, tbl_13, tbl_14, tbl_15, tbl_16, tbl_17, tbl_18, tbl_19, tbl_20, tbl_21, tbl_22, tbl_23, tbl_24, tbl_25, W_top1, b_top1, W_top2, b_top2, W_top3):
    import jax
    import jax.numpy as jnp

    def _L0_rec_ref(dense_features, sparse_features):
        import jax, jax.numpy as jnp
        import numpy as np
        NUM_SPARSE = 26
        EMBED_DIM = 128
        BATCH = 2048
        F = NUM_SPARSE + 1
        combined = jnp.concatenate([dense_features[:, None, :], sparse_features], axis=1)
        interactions = jnp.einsum('bfd,bgd->bfg', combined, combined)
        iu, ju = jnp.triu_indices(F, k=1)
        interactions_flat = interactions[:, iu, ju]
        return jnp.concatenate([dense_features, interactions_flat], axis=1)
    e = jnp.stack([tbl_0[ids[:, 0]], tbl_1[ids[:, 1]], tbl_2[ids[:, 2]], tbl_3[ids[:, 3]], tbl_4[ids[:, 4]], tbl_5[ids[:, 5]], tbl_6[ids[:, 6]], tbl_7[ids[:, 7]], tbl_8[ids[:, 8]], tbl_9[ids[:, 9]], tbl_10[ids[:, 10]], tbl_11[ids[:, 11]], tbl_12[ids[:, 12]], tbl_13[ids[:, 13]], tbl_14[ids[:, 14]], tbl_15[ids[:, 15]], tbl_16[ids[:, 16]], tbl_17[ids[:, 17]], tbl_18[ids[:, 18]], tbl_19[ids[:, 19]], tbl_20[ids[:, 20]], tbl_21[ids[:, 21]], tbl_22[ids[:, 22]], tbl_23[ids[:, 23]], tbl_24[ids[:, 24]], tbl_25[ids[:, 25]]], axis=1)
    z = _L0_rec_ref(r_dense_features, e)
    z = z.reshape(z.shape[0], -1)
    h = jnp.concatenate([z, r_dense_features], axis=1)
    h = jnp.maximum(h @ W_top1 + b_top1, 0.0)
    h = jnp.maximum(h @ W_top2 + b_top2, 0.0)
    y = h @ W_top3
    return y

_drawn_inputs = setup_inputs


def setup_inputs(seed=0):
    import zlib

    import numpy as np

    out = dict(_drawn_inputs(seed))
    spreads = {'b_top1': (0.0, 0.1), 'b_top2': (0.0, 0.1)}
    factors = {}
    for name, (base, spread) in spreads.items():
        noise = np.random.default_rng([zlib.crc32(name.encode()), seed]).standard_normal(out[name].shape)
        drawn = base * np.exp(spread * noise) if base else spread * noise
        out[name] = jnp.asarray(drawn.astype(out[name].dtype))
    for name, factor in factors.items():
        out[name] = (out[name] * factor).astype(out[name].dtype)
    return out
```

```python
from concourse import mybir
import concourse.bass as bass

F32 = mybir.dt.float32
F32R = mybir.dt.float32r
I32 = mybir.dt.int32
ALU = mybir.AluOpType
ACT = mybir.ActivationFunctionType

P = 128
BATCH = 2048
D = 128
TABLES = 26
F = TABLES + 1
SUBS = 2
TILE = SUBS * P
TILES = BATCH // TILE
HIDDEN1, HIDDEN2 = 512, 256
N1, N2 = HIDDEN1 // P, HIDDEN2 // P

ONEHOT = [1, 4, 6, 7, 10, 11, 12, 13]
GATHERED = [n for n in range(TABLES) if n not in ONEHOT]
NO, NG = len(ONEHOT), len(GATHERED)
ROWS = 1000
KC = 8
KR = ROWS // KC
HALF = KC // 2
SPRAY = KR // 16 * 16

ORDER = [0] + [1 + n for n in GATHERED] + [1 + n for n in ONEHOT]
DENSE = 0
SENT = 1 + NG
GROUP = 4
GROUPS = [(a, min(a + GROUP, SENT)) for a in range(0, SENT, GROUP)]
GT = SUBS * len(GROUPS)

QUAD = 32
QUADS = P // QUAD
BANK_I = 16
SUBW = P * F + QUAD - F
SHIFTS = F // 2
PAIRS = SHIFTS * F
ZC = -(-PAIRS // P)
ZROWS = [min(P, PAIRS - c * P) for c in range(ZC)]
WIDE = F + SHIFTS
RUN = SUBS * QUAD


def z_loads():
    out = []
    for s in range(1, SHIFTS + 1):
        p = 0
        while p < F:
            q = (s - 1) * F + p
            n = min(F - p, P - q % P)
            out.append((s, p, n, q // P, q % P))
            p += n
    return out


Z_LOADS = z_loads()


def tower(nc, dense, ids_rows, ids_flat, tables, w1, w2, columns_in, y):
    from contextlib import ExitStack

    ctx = ExitStack()
    with ctx:
        def sb(name, shape, dt=F32):
            return ctx.enter_context(nc.sbuf_tensor(name, shape, dt))

        def ps(name, shape):
            return ctx.enter_context(nc.psum_tensor(name, shape, F32))

        def sem(name):
            return ctx.enter_context(nc.semaphore(name))

        ident = sb("ident", [P, P])
        ids_sb = sb("ids_sb", [P, BATCH // P, TABLES], I32)
        ids_now = sb("ids_now", [P, SUBS, TABLES], I32)
        rowid = sb("rowid", [P, KC])
        ids_oh = sb("ids_oh", [P, NO, TILE], I32)
        onehot = sb("onehot", [P, 2, KC, TILE], F32R)
        tab_hi = sb("tab_hi", [P, NO, KC, D], F32R)
        tab_lo = sb("tab_lo", [P, NO, KC, D], F32R)
        raw = sb("raw", [P, 2, KC * D])
        rows = sb("rows", [P, SUBS, SENT, D])
        ct = sb("ct", [P, SUBS, SUBW])
        gram = sb("gram", [P, F, RUN])
        z = sb("z", [P, ZC, TILE])
        z_hi = sb("z_hi", [P, ZC, TILE], F32R)
        z_lo = sb("z_lo", [P, ZC, TILE], F32R)
        d_hi = sb("d_hi", [P, TILE], F32R)
        d_lo = sb("d_lo", [P, TILE], F32R)
        w1_hi = sb("w1_hi", [P, ZC + 1, HIDDEN1], F32R)
        w1_lo = sb("w1_lo", [P, ZC + 1, HIDDEN1], F32R)
        w2_hi = sb("w2_hi", [P, N1, HIDDEN2], F32R)
        w2_lo = sb("w2_lo", [P, N1, HIDDEN2], F32R)
        columns = sb("columns", [P, N1 + 2 * N2])
        b1_sb, b2_sb, w3_sb = columns[:, 0:N1], columns[:, N1:N1 + N2], columns[:, N1 + N2:N1 + 2 * N2]
        h1 = sb("h1", [P, N1, TILE])
        h1_hi = sb("h1_hi", [P, N1, TILE], F32R)
        h1_lo = sb("h1_lo", [P, N1, TILE], F32R)
        h2 = sb("h2", [P, N2, TILE])
        y_sb = sb("y_sb", [1, TILE])

        ps_t = ps("ps_t", [P, 2, GROUP * P])
        ps_o = ps("ps_o", [P, 2, 512])
        ps_g = ps("ps_g", [P, 2, 512])
        ps_m = ps("ps_m", [P, 2, 2, TILE])

        scratch = nc.dram_tensor("scratch", [P, WIDE, RUN], F32, kind="Internal")

        ids_landed = sem("ids_landed")
        raw_landed = [sem(f"raw_landed{n}") for n in range(2)]
        raw_split = sem("raw_split")
        columns_landed = sem("columns_landed")
        ids_oh_landed = sem("ids_oh_landed")
        dense_landed = [sem(f"dense_landed{s}") for s in range(SUBS)]
        rows_landed = [sem(f"rows_landed{s}") for s in range(SUBS)]
        zeroed = sem("zeroed")
        consts_made = sem("consts_made")
        ids_taken = sem("ids_taken")
        gathers_begun = sem("gathers_begun")
        parts_high = sem("parts_high")
        weights_split = sem("weights_split")
        onehots_made = sem("onehots_made")
        transposed = sem("transposed")
        transposes_saved = sem("transposes_saved")
        looked_up = sem("looked_up")
        lookups_saved = sem("lookups_saved")
        gram_done = sem("gram_done")
        gram_saved = sem("gram_saved")
        scratch_written = sem("scratch_written")
        z_landed = sem("z_landed")
        z_split = sem("z_split")
        dense_split = sem("dense_split")
        layer1_done = sem("layer1_done")
        h1_saved = sem("h1_saved")
        h1_split = sem("h1_split")
        layer2_done = sem("layer2_done")
        h2_saved = sem("h2_saved")
        layer3_done = sem("layer3_done")
        y_saved = sem("y_saved")
        y_stored = sem("y_stored")

        items = []
        for n in ONEHOT:
            table = tables[n].rearrange("(p c) d -> p (c d)", c=KC)
            items.append([(0, SPRAY, 0, KC * D, table[0:SPRAY]), (SPRAY, KR, 0, KC * D, table[SPRAY:KR])])
        w1_pairs = w1[D:D + PAIRS]
        items.append([(0, ZROWS[c], c * HIDDEN1, (c + 1) * HIDDEN1, w1_pairs[c * P:c * P + ZROWS[c]])
                      for c in (0, 1)])
        items.append([(0, ZROWS[2], 0, HIDDEN1, w1_pairs[2 * P:PAIRS])])
        items.append([(0, P, 0, HIDDEN1, w1[0:D]), (0, P, HIDDEN1, 2 * HIDDEN1, w1[D + PAIRS:2 * D + PAIRS])])
        items.append([(0, P, c * HIDDEN2, (c + 1) * HIDDEN2, w2[c * P:(c + 1) * P]) for c in range(N1)])
        ITEM_W1, ITEM_W1_LAST, ITEM_DENSE, ITEM_W2 = range(NO, NO + 4)

        def raw_count(n):
            return 16 * sum(len(items[m]) for m in range(n % 2, n + 1, 2))

        block = ctx.enter_context(nc.Block())

        @block.sync
        def _(sp):
            sp.dma_start(ids_sb[:, :, :], ids_rows).then_inc(ids_landed, 16)

            def stage(n):
                if n >= 2:
                    sp.wait_ge(raw_split, n - 1)
                for p0, p1, c0, c1, source in items[n]:
                    sp.dma_start(raw[p0:p1, n % 2, c0:c1], source).then_inc(raw_landed[n % 2], 16)

            def load_dense(s, t):
                sp.dma_start(rows[:, s, DENSE, :], dense[bass.ds(t * SUBS + s, 1)]
                             .rearrange("o p d -> (o p) d")).then_inc(dense_landed[s], 16)

            def load_ids_oh(t):
                sp.dma_start(ids_oh[:, :, :].rearrange("p n b -> p (n b)"),
                             ids_flat[bass.ds(t, 1)].rearrange("o n -> (o n)")
                             .partition_broadcast(P)).then_inc(ids_oh_landed, 16)

            def collect_pairs(t, first):
                if not first:
                    sp.wait_ge(z_landed, t * (16 * len(Z_LOADS)))
                sp.wait_ge(gram_saved, t * SUBS + SUBS)
                sp.dma_start(scratch[:, 0:F, :], gram[:, :, :]).then_inc(scratch_written, 16)
                sp.dma_start(scratch[:, F:WIDE, :], gram[:, 0:SHIFTS, :]).then_inc(scratch_written, 16)
                sp.wait_ge(scratch_written, t * 32 + 32)
                if not first:
                    sp.wait_ge(z_split, t)
                for s, p, n, c, q in Z_LOADS:
                    source = bass.AP(scratch, (p * WIDE + p + s) * RUN,
                                     [[(WIDE + 1) * RUN, n], [QUAD * WIDE * RUN, QUADS], [1, RUN]])
                    sp.dma_start(z[q:q + n, c, :].rearrange("p (j r) -> p j r", j=QUADS),
                                 source).then_inc(z_landed, 16)

            def store_y(t):
                sp.wait_ge(y_saved, t + 1)
                sp.dma_start(y.rearrange("(t s j i) o -> t o j s i", t=TILES, s=SUBS, j=QUADS)
                             [bass.ds(t, 1)].rearrange("t o j s i -> (t o) j s i"),
                             y_sb[:, :].rearrange("o (j s i) -> o j s i", j=QUADS, s=SUBS)
                             ).then_inc(y_stored, 16)

            stage(0)
            load_ids_oh(0)
            stage(1)
            for s in range(SUBS):
                load_dense(s, 0)
            sp.dma_start(columns[:, :], columns_in).then_inc(columns_landed, 16)
            for n in range(2, len(items)):
                stage(n)
            def tile(t, first, last):
                if not last:
                    sp.wait_ge(onehots_made, t * (2 * NO) + 2 * NO)
                    load_ids_oh(t + 1)
                    for s in range(SUBS):
                        sp.wait_ge(transposed, t * GT + (s + 1) * len(GROUPS))
                        load_dense(s, t + 1)
                collect_pairs(t, first)
                if not first:
                    store_y(t - 1)

            tile(0, True, False)
            with sp.Fori(1, TILES - 1) as t:
                tile(t, False, False)
            tile(TILES - 1, False, True)
            store_y(TILES - 1)
            sp.wait_ge(y_stored, 16 * TILES)

        @block.gpsimd
        def _(pool):
            pool.iota(rowid[:, :], [[1, KC]], base=0, channel_multiplier=KC,
                      allow_small_or_imprecise_dtypes=True).then_inc(consts_made, 1)
            pool.memset(ident[:, :], 0.0).then_inc(zeroed, 1)
            pool.wait_ge(zeroed, 1)
            pool.affine_select(out=ident[:, :], in_=ident[:, :], compare_op=ALU.not_equal, fill=1.0, base=0,
                               pattern=[[-1, P]], channel_multiplier=1).then_inc(consts_made, 1)
            pool.wait_ge(ids_landed, 16)

            def tile(t, first):
                for s in range(SUBS):
                    if not first:
                        pool.wait_ge(transposed, t * GT - (SUBS - 1 - s) * len(GROUPS))
                    pool.tensor_copy(ids_now[:, s, :], ids_sb[:, bass.ds(t * SUBS + s, 1), :]
                                     .rearrange("p o f -> p (o f)")).then_inc(ids_taken, 1)
                    pool.wait_ge(ids_taken, t * SUBS + s + 1)
                    pool.sem_inc(gathers_begun, 1)
                    for k, n in enumerate(GATHERED):
                        pool.indirect_dma_start(rows[:, s, 1 + k, :], None, tables[n],
                                                bass.IndirectOffsetOnAxis(ap=ids_now[:, s, n:n + 1], axis=0)
                                                ).then_inc(rows_landed[s], 16)

            tile(0, True)
            with pool.Fori(1, TILES) as t:
                tile(t, False)

        @block.tensor
        def _(pe):
            def transposes(t, s, first):
                pe.wait_ge(rows_landed[s], t * (16 * NG) + 16 * NG)
                pe.wait_ge(dense_landed[s], t * 16 + 16)
                for g, (a, b) in enumerate(GROUPS):
                    n = s * len(GROUPS) + g
                    if not (first and n < 2):
                        pe.wait_ge(transposes_saved, t * GT + (n - 1))
                    for f in range(a, b):
                        mm = pe.transpose(ps_t[:, n % 2, (f - a) * P:(f - a + 1) * P], rows[:, s, f, :], ident[:, :])
                    mm.then_inc(transposed, 1)

            def lookups(t, first):
                for k in range(NO):
                    if first:
                        pe.wait_ge(raw_split, k + 1)
                    if not (first and k < 2):
                        pe.wait_ge(lookups_saved, t * NO + (k - 1))
                    for c in range(KC):
                        if c % HALF == 0:
                            pe.wait_ge(onehots_made, t * (2 * NO) + 2 * k + c // HALF + 1)
                        for part, tab in enumerate((tab_hi, tab_lo)):
                            mm = pe.matmul(ps_o[:, k % 2, 0:TILE], tab[0:KR, k, c, :], onehot[0:KR, k % 2, c, :],
                                           start=(c == 0 and part == 0), stop=(c == KC - 1 and part == 1))
                    mm.then_inc(looked_up, 1)

            def dot_products(t, s, first):
                pe.wait_ge(transposes_saved, t * GT + (s + 1) * len(GROUPS))
                pe.wait_ge(lookups_saved, t * NO + NO)
                if not (first and s == 0):
                    pe.wait_ge(gram_saved, t * SUBS + s)
                for i in range(QUAD):
                    for j in range(QUADS):
                        at = (j * QUAD + i) * F
                        mm = pe.matmul(ps_g[j * QUAD:(j + 1) * QUAD, i // BANK_I,
                                            i % BANK_I * F:(i % BANK_I + 1) * F],
                                       ct[:, s, at:at + QUAD], ct[:, s, at:at + F],
                                       start=True, stop=True, skip_group_check=True)
                mm.then_inc(gram_done, 1)

            def layer(out, chunks):
                for c, (w_hi, w_lo, x_hi, x_lo) in enumerate(chunks):
                    for m, (w, x) in enumerate(((w_hi, x_hi), (w_hi, x_lo), (w_lo, x_hi))):
                        mm = pe.matmul(out, w, x, start=(c == 0 and m == 0), stop=(c == len(chunks) - 1 and m == 2))
                return mm

            def layer1(t, first):
                if first:
                    pe.wait_ge(weights_split, 1)
                else:
                    pe.wait_ge(y_saved, t)
                pe.wait_ge(dense_split, t + 1)
                pe.wait_ge(z_split, t + 1)
                for n in range(N1):
                    cols = slice(n * P, (n + 1) * P)
                    chunks = [(w1_hi[:, ZC, cols], w1_lo[:, ZC, cols], d_hi[:, :], d_lo[:, :])]
                    for c, k in enumerate(ZROWS):
                        chunks.append((w1_hi[0:k, c, cols], w1_lo[0:k, c, cols], z_hi[0:k, c, :], z_lo[0:k, c, :]))
                    mm = layer(ps_m[:, n // 2, n % 2, :], chunks)
                    if n % 2 == 1:
                        mm.then_inc(layer1_done, 1)

            def layer2(t):
                pe.wait_ge(h1_split, t + 1)
                for n in range(N2):
                    cols = slice(n * P, (n + 1) * P)
                    mm = layer(ps_m[:, 0, n, :], [(w2_hi[:, c, cols], w2_lo[:, c, cols], h1_hi[:, c, :],
                                                   h1_lo[:, c, :]) for c in range(N1)])
                mm.then_inc(layer2_done, 1)

            def layer3(t):
                pe.wait_ge(h2_saved, t * N2 + N2)
                for c in range(N2):
                    mm = pe.matmul(ps_m[0:1, 1, 0, :], w3_sb[:, c:c + 1], h2[:, c, :], start=(c == 0), stop=(c == N2 - 1))
                mm.then_inc(layer3_done, 1)

            pe.wait_ge(consts_made, 2)
            lookups(0, True)
            transposes(0, 0, True)
            dot_products(0, 0, True)
            transposes(0, 1, True)
            dot_products(0, 1, True)

            def tile(t, first_mlp):
                transposes(t, 0, False)
                lookups(t, False)
                dot_products(t, 0, False)
                transposes(t, 1, False)
                layer1(t - 1, first_mlp)
                dot_products(t, 1, False)
                layer2(t - 1)
                layer3(t - 1)

            pe.wait_ge(columns_landed, 16)
            tile(1, True)
            with pe.Fori(2, TILES) as t:
                tile(t, False)
            layer1(TILES - 1, False)
            layer2(TILES - 1)
            layer3(TILES - 1)

        @block.scalar
        def _(act):
            def save_transposes(t, s, first):
                if not first and s == 0:
                    act.wait_ge(dense_split, t)
                for g, (a, b) in enumerate(GROUPS):
                    n = s * len(GROUPS) + g
                    act.wait_ge(transposed, t * GT + n + 1)
                    act.activation(ct[:, s, 0:P * F].rearrange("p (b f) -> p b f", f=F)[:, :, a:b],
                                   ps_t[:, n % 2, 0:(b - a) * P].rearrange("p (f b) -> p b f", b=P),
                                   ACT.Copy).then_inc(transposes_saved, 1)

            def save_lookups(t):
                for k in range(NO):
                    act.wait_ge(looked_up, t * NO + k + 1)
                    act.activation(ct[:, :, 0:P * F].rearrange("p s (b f) -> p s b f", f=F)[:, :, :, SENT + k],
                                   ps_o[:, k % 2, 0:TILE].rearrange("p (s b) -> p s b", s=SUBS),
                                   ACT.Copy).then_inc(lookups_saved, 1)

            def save_gram(t, s, first):
                act.wait_ge(gram_done, t * SUBS + s + 1)
                if not first and s == 0:
                    act.wait_ge(scratch_written, t * 32)
                act.activation(gram[:, :, :].rearrange("p g (s c i) -> p s c i g", s=SUBS, c=2)[:, s],
                               ps_g[:, :, 0:BANK_I * F].rearrange("p c (i g) -> p c i g", g=F),
                               ACT.Copy).then_inc(gram_saved, 1)

            def save_h1(t, first):
                if first:
                    act.wait_ge(columns_landed, 16)
                else:
                    act.wait_ge(h1_split, t)
                for n in range(N1):
                    if n % 2 == 0:
                        act.wait_ge(layer1_done, t * (N1 // 2) + n // 2 + 1)
                    act.activation(h1[:, n, :], ps_m[:, n // 2, n % 2, :], ACT.Relu,
                                   bias=b1_sb[:, n:n + 1]).then_inc(h1_saved, 1)

            def save_h2(t):
                act.wait_ge(layer2_done, t + 1)
                for n in range(N2):
                    act.activation(h2[:, n, :], ps_m[:, 0, n, :], ACT.Relu,
                                   bias=b2_sb[:, n:n + 1]).then_inc(h2_saved, 1)

            def save_y(t, first):
                act.wait_ge(layer3_done, t + 1)
                if not first:
                    act.wait_ge(y_stored, t * 16)
                act.activation(y_sb[:, :], ps_m[0:1, 1, 0, :], ACT.Copy).then_inc(y_saved, 1)

            save_lookups(0)
            for s in range(SUBS):
                save_transposes(0, s, True)
                save_gram(0, s, True)

            def tile(t, first_mlp):
                save_transposes(t, 0, False)
                save_lookups(t)
                save_gram(t, 0, False)
                save_transposes(t, 1, False)
                save_h1(t - 1, first_mlp)
                save_gram(t, 1, False)
                save_h2(t - 1)
                save_y(t - 1, first_mlp)

            tile(1, True)
            with act.Fori(2, TILES) as t:
                tile(t, False)
            save_h1(TILES - 1, False)
            save_h2(TILES - 1)
            save_y(TILES - 1, False)

        @block.vector
        def _(dve):
            highs = [0]

            def split(high, low, source, waited=None):
                dve.tensor_copy(high, source).then_inc(parts_high, 1)
                highs[0] += 1
                dve.wait_ge(parts_high, highs[0] if waited is None else waited)
                return dve.tensor_tensor(low, source, high, ALU.subtract)

            def split_table(k):
                dve.wait_ge(raw_landed[k % 2], raw_count(k))
                split(tab_hi[0:KR, k, :, :].rearrange("p c d -> p (c d)"),
                      tab_lo[0:KR, k, :, :].rearrange("p c d -> p (c d)"),
                      raw[0:KR, k % 2, :]).then_inc(raw_split, 1)

            def onehots(t, first):
                dve.wait_ge(ids_oh_landed, t * 16 + 16)
                for k in range(NO):
                    if first:
                        split_table(k)
                    if not (first and k < 2):
                        dve.wait_ge(looked_up, t * NO + (k - 1))
                    for c in range(KC):
                        mm = dve.tensor_scalar(onehot[:, k % 2, c, :], ids_oh[:, k, :], rowid[:, c:c + 1],
                                               None, ALU.is_equal)
                        if c % HALF == HALF - 1:
                            mm.then_inc(onehots_made, 1)

            def split_weights():
                for item, c0, nc_ in ((ITEM_W1, 0, 2), (ITEM_W1_LAST, 2, 1)):
                    dve.wait_ge(raw_landed[item % 2], raw_count(item))
                    k = ZROWS[c0]
                    split(w1_hi[0:k, c0:c0 + nc_, :].rearrange("p c n -> p (c n)"),
                          w1_lo[0:k, c0:c0 + nc_, :].rearrange("p c n -> p (c n)"),
                          raw[0:k, item % 2, 0:nc_ * HIDDEN1]).then_inc(raw_split, 1)
                item = ITEM_DENSE
                dve.wait_ge(raw_landed[item % 2], raw_count(item))
                both = h1[:, 0:2, :].rearrange("p c n -> p (c n)")
                dve.tensor_tensor(both, raw[:, item % 2, 0:HIDDEN1], raw[:, item % 2, HIDDEN1:2 * HIDDEN1],
                                  ALU.add).then_inc(raw_split, 1)
                dve.wait_ge(raw_split, item + 1)
                split(w1_hi[:, ZC, :], w1_lo[:, ZC, :], both)
                item = ITEM_W2
                dve.wait_ge(raw_landed[item % 2], raw_count(item))
                split(w2_hi[:, :, :].rearrange("p c n -> p (c n)"), w2_lo[:, :, :].rearrange("p c n -> p (c n)"),
                      raw[:, item % 2, :]).then_inc(weights_split, 1)

            def split_z(t, first):
                dve.wait_ge(z_landed, t * (16 * len(Z_LOADS)) + 16 * len(Z_LOADS))
                if not first:
                    dve.wait_ge(layer1_done, t * (N1 // 2))
                base = t * 4 + PARTS + 1
                full = ZC - 1
                k = ZROWS[full]
                split(z_hi[:, 0:full, :], z_lo[:, 0:full, :], z[:, 0:full, :], base)
                split(z_hi[0:k, full, :], z_lo[0:k, full, :], z[0:k, full, :], base + 1).then_inc(z_split, 1)

            def split_h1(t):
                dve.wait_ge(h1_saved, t * N1 + N1)
                split(h1_hi[:, :, :], h1_lo[:, :, :], h1[:, :, :], t * 4 + PARTS + 3).then_inc(h1_split, 1)

            def split_dense(t, first, count):
                dve.wait_ge(transposes_saved, t * GT + (GT - len(GROUPS) + 1))
                if not first:
                    dve.wait_ge(layer1_done, t * (N1 // 2))
                view = ct[:, :, 0:P * F].rearrange("p s (j i f) -> p j s i f", j=QUADS, f=F)[:, :, :, :, DENSE]
                shape = "p (j s i) -> p j s i"
                split(d_hi[:, :].rearrange(shape, j=QUADS, s=SUBS), d_lo[:, :].rearrange(shape, j=QUADS, s=SUBS),
                      view, count).then_inc(dense_split, 1)

            dve.memset(ct[:, :, P * F:SUBW], 0.0).then_inc(parts_high, 1)
            highs[0] += 1
            dve.wait_ge(consts_made, 1)
            onehots(0, True)
            split_weights()
            split_dense(0, True, None)
            PARTS = highs[0]

            def tile(t, first_mlp):
                onehots(t, False)
                split_z(t - 1, first_mlp)
                split_h1(t - 1)
                split_dense(t, False, (t - 1) * 4 + PARTS + 4)

            tile(1, True)
            with dve.Fori(2, TILES) as t:
                tile(t, False)
            split_z(TILES - 1, False)
            split_h1(TILES - 1)


def kernel(**inputs):
    import numpy as np
    import concourse.bacc as bacc
    from concourse.bass_utils import run_bass_kernel_spmd as run

    nc = bacc.Bacc("TRN2", target_bir_lowering=False, num_devices=1)
    host = {k: np.asarray(v) for k, v in inputs.items()}
    natural = {}
    for a in range(F):
        for b in range(a + 1, F):
            natural[a, b] = len(natural)
    order = []
    for s in range(1, SHIFTS + 1):
        for p in range(F):
            a, b = ORDER[p], ORDER[(p + s) % F]
            order.append(natural[min(a, b), max(a, b)])
    w1_rows = np.array([*range(D), *(D + q for q in order), *range(D + PAIRS, 2 * D + PAIRS)])
    ids = host["ids"]
    arrays = {
        "dense": host["r_dense_features"].reshape(BATCH // P, P, D),
        "ids_rows": ids.reshape(BATCH // P, P, TABLES).transpose(1, 0, 2),
        "ids_flat": ids[:, ONEHOT].reshape(TILES, TILE, NO).transpose(0, 2, 1).reshape(TILES, NO * TILE),
        "w1": host["W_top1"][w1_rows],
        "w2": host["W_top2"],
        "columns": np.concatenate([host["b_top1"].reshape(N1, P), host["b_top2"].reshape(N2, P),
                                   host["W_top3"].reshape(N2, P)]).T,
    }
    arrays |= {f"tbl_{n}": host[f"tbl_{n}"] for n in range(TABLES)}
    arrays = {k: np.ascontiguousarray(a) for k, a in arrays.items()}
    arrays = {f"in_{k}": a for k, a in arrays.items()}
    aps = {k[3:]: nc.dram_tensor(k, a.shape, mybir.dt.from_np(a.dtype), kind="ExternalInput").ap()
           for k, a in arrays.items()}
    y = nc.dram_tensor("y", (BATCH, 1), F32, kind="ExternalOutput").ap()
    tables = [aps[f"tbl_{n}"] for n in range(TABLES)]
    tower(nc, aps["dense"], aps["ids_rows"], aps["ids_flat"], tables, aps["w1"], aps["w2"],
          aps["columns"], y)
    return run(nc, [arrays], core_ids=[0]).results[0]["y"]
```

```python
from concourse import mybir
import concourse.bass as bass

F32 = mybir.dt.float32
F32R = mybir.dt.float32r
I32 = mybir.dt.int32
ALU = mybir.AluOpType
ACT = mybir.ActivationFunctionType

P = 128
BATCH = 2048
D = 128
TABLES = 26
F = TABLES + 1
SUBS = 2
TILE = SUBS * P
TILES = BATCH // TILE
HIDDEN1, HIDDEN2 = 512, 256
N1, N2 = HIDDEN1 // P, HIDDEN2 // P

ONEHOT = [1, 4, 6, 7, 10, 11, 12, 13]
GATHERED = [n for n in range(TABLES) if n not in ONEHOT]
NO, NG = len(ONEHOT), len(GATHERED)
ROWS = 1000
KC = 8
KR = ROWS // KC
HALF = KC // 2
HALVES = 2 * NO
RING = 4
assert HALVES % RING == 0
SPRAY = KR // 16 * 16

ORDER = [0] + [1 + n for n in GATHERED] + [1 + n for n in ONEHOT]
DENSE = 0
SENT = 1 + NG
GROUP = 4
GROUPS = [(a, min(a + GROUP, SENT)) for a in range(0, SENT, GROUP)]
GT = SUBS * len(GROUPS)
ALONE = NO - len(GROUPS)

QUAD = 32
QUADS = P // QUAD
BANK_I = 16
SUBW = P * F + QUAD - F
SHIFTS = F // 2
PAIRS = SHIFTS * F
ZC = -(-PAIRS // P)
ZROWS = [min(P, PAIRS - c * P) for c in range(ZC)]
WIDE = F + SHIFTS
RUN = SUBS * QUAD


def z_loads():
    out = []
    for s in range(1, SHIFTS + 1):
        p = 0
        while p < F:
            q = (s - 1) * F + p
            n = min(F - p, P - q % P)
            out.append((s, p, n, q // P, q % P))
            p += n
    return out


Z_LOADS = z_loads()
Z_OF = [sum(load[3] == c for load in Z_LOADS) for c in range(ZC)]


def tower(nc, dense, ids_rows, ids_flat, tables, w1, w2, columns_in, y):
    from contextlib import ExitStack

    ctx = ExitStack()
    with ctx:
        def sb(name, shape, dt=F32):
            return ctx.enter_context(nc.sbuf_tensor(name, shape, dt))

        def ps(name, shape):
            return ctx.enter_context(nc.psum_tensor(name, shape, F32))

        def sem(name):
            return ctx.enter_context(nc.semaphore(name))

        ident = sb("ident", [P, P])
        ids_sb = sb("ids_sb", [P, BATCH // P, NG], I32)
        ids_now = sb("ids_now", [P, SUBS, NG], I32)
        rowid = sb("rowid", [P, KC])
        ids_oh = sb("ids_oh", [P, NO, TILE], I32)
        onehot = sb("onehot", [P, RING, HALF, TILE], F32R)
        tab_hi = sb("tab_hi", [P, NO, KC, D], F32R)
        tab_lo = sb("tab_lo", [P, NO, KC, D], F32R)
        raw = sb("raw", [P, 2, KC * D])
        rows = sb("rows", [P, SUBS, SENT, D])
        ct = sb("ct", [P, SUBS, SUBW])
        gram = sb("gram", [P, F, RUN])
        z = sb("z", [P, ZC, TILE])
        z_hi = sb("z_hi", [P, ZC, TILE], F32R)
        z_lo = sb("z_lo", [P, ZC, TILE], F32R)
        d_hi = sb("d_hi", [P, TILE], F32R)
        d_lo = sb("d_lo", [P, TILE], F32R)
        w1_hi = sb("w1_hi", [P, ZC + 1, HIDDEN1], F32R)
        w1_lo = sb("w1_lo", [P, ZC + 1, HIDDEN1], F32R)
        w2_hi = sb("w2_hi", [P, N1, HIDDEN2], F32R)
        w2_lo = sb("w2_lo", [P, N1, HIDDEN2], F32R)
        columns = sb("columns", [P, N1 + 2 * N2])
        b1_sb, b2_sb, w3_sb = columns[:, 0:N1], columns[:, N1:N1 + N2], columns[:, N1 + N2:N1 + 2 * N2]
        h1 = sb("h1", [P, N1, TILE])
        h1_hi = sb("h1_hi", [P, N1, TILE], F32R)
        h1_lo = sb("h1_lo", [P, N1, TILE], F32R)
        h2 = sb("h2", [P, N2, TILE])
        y_sb = sb("y_sb", [1, BATCH])

        ps_t = ps("ps_t", [P, 2, GROUP * P])
        ps_o = ps("ps_o", [P, 2, 512])
        ps_g = ps("ps_g", [P, 2, 512])
        ps_m = ps("ps_m", [P, 2, 2, TILE])

        scratch = nc.dram_tensor("scratch", [P, WIDE, RUN], F32, kind="Internal")

        ids_landed = sem("ids_landed")
        raw_landed = [sem(f"raw_landed{n}") for n in range(2)]
        raw_split = sem("raw_split")
        columns_landed = sem("columns_landed")
        ids_oh_landed = sem("ids_oh_landed")
        dense_landed = [sem(f"dense_landed{s}") for s in range(SUBS)]
        rows_landed = [[sem(f"rows_landed{s}_{g}") for g in range(len(GROUPS))] for s in range(SUBS)]
        zeroed = sem("zeroed")
        consts_made = sem("consts_made")
        ids_taken = sem("ids_taken")
        table_highs = sem("table_highs")
        gathers_begun = sem("gathers_begun")
        parts_high = sem("parts_high")
        weights_split = sem("weights_split")
        onehots_made = sem("onehots_made")
        transposed = sem("transposed")
        transposes_saved = sem("transposes_saved")
        looked_up = sem("looked_up")
        lookups_saved = sem("lookups_saved")
        gram_done = sem("gram_done")
        gram_saved = sem("gram_saved")
        scratch_written = sem("scratch_written")
        z_landed = [sem(f"z_landed{c}") for c in range(ZC)]
        z_split = sem("z_split")
        dense_split = sem("dense_split")
        layer1_done = sem("layer1_done")
        h1_saved = sem("h1_saved")
        h1_split = sem("h1_split")
        layer2_done = sem("layer2_done")
        h2_saved = sem("h2_saved")
        layer3_done = sem("layer3_done")
        y_saved = sem("y_saved")
        y_stored = sem("y_stored")

        items = []
        for n in ONEHOT:
            table = tables[n].rearrange("(p c) d -> p (c d)", c=KC)
            items.append([(0, SPRAY, 0, KC * D, table[0:SPRAY]), (SPRAY, KR, 0, KC * D, table[SPRAY:KR])])
        w1_pairs = w1[D:D + PAIRS]
        items.append([(0, ZROWS[c], c * HIDDEN1, (c + 1) * HIDDEN1, w1_pairs[c * P:c * P + ZROWS[c]])
                      for c in (0, 1)])
        items.append([(0, ZROWS[2], 0, HIDDEN1, w1_pairs[2 * P:PAIRS])])
        items.append([(0, P, 0, HIDDEN1, w1[0:D]), (0, P, HIDDEN1, 2 * HIDDEN1, w1[D + PAIRS:2 * D + PAIRS])])
        items.append([(0, P, c * HIDDEN2, (c + 1) * HIDDEN2, w2[c * P:(c + 1) * P]) for c in range(N1)])
        ITEM_W1, ITEM_W1_LAST, ITEM_DENSE, ITEM_W2 = range(NO, NO + 4)

        def raw_count(n):
            return 16 * sum(len(items[m]) for m in range(n % 2, n + 1, 2))

        block = ctx.enter_context(nc.Block())

        @block.sync
        def _(sp):
            sp.dma_start(ids_sb[:, :, :], ids_rows).then_inc(ids_landed, 16)

            def stage(n):
                if n >= 2:
                    sp.wait_ge(raw_split, n - 1)
                for p0, p1, c0, c1, source in items[n]:
                    sp.dma_start(raw[p0:p1, n % 2, c0:c1], source).then_inc(raw_landed[n % 2], 16)

            def load_dense(s, t):
                sp.dma_start(rows[:, s, DENSE, :], dense[bass.ds(t * SUBS + s, 1)]
                             .rearrange("o p d -> (o p) d")).then_inc(dense_landed[s], 16)

            def load_ids_oh(t):
                sp.dma_start(ids_oh[:, :, :].rearrange("p n b -> p (n b)"),
                             ids_flat[bass.ds(t, 1)].rearrange("o n -> (o n)")
                             .partition_broadcast(P)).then_inc(ids_oh_landed, 16)

            def collect_pairs(t, first):
                if not first:
                    sp.wait_ge(z_split, t * ZC)
                sp.wait_ge(gram_saved, t * SUBS + SUBS)
                sp.dma_start(scratch[:, 0:F, :], gram[:, :, :]).then_inc(scratch_written, 16)
                sp.dma_start(scratch[:, F:WIDE, :], gram[:, 0:SHIFTS, :]).then_inc(scratch_written, 16)
                sp.wait_ge(scratch_written, t * 32 + 32)
                for s, p, n, c, q in Z_LOADS:
                    source = bass.AP(scratch, (p * WIDE + p + s) * RUN,
                                     [[(WIDE + 1) * RUN, n], [QUAD * WIDE * RUN, QUADS], [1, RUN]])
                    sp.dma_start(z[q:q + n, c, :].rearrange("p (j r) -> p j r", j=QUADS),
                                 source).then_inc(z_landed[c], 16)

            stage(0)
            load_ids_oh(0)
            stage(1)
            for s in range(SUBS):
                load_dense(s, 0)
            sp.dma_start(columns[:, :], columns_in).then_inc(columns_landed, 16)
            for n in range(2, len(items)):
                stage(n)
            def tile(t, first, last):
                if not last:
                    sp.wait_ge(onehots_made, t * HALVES + HALVES)
                    load_ids_oh(t + 1)
                    for s in range(SUBS):
                        sp.wait_ge(transposed, t * GT + (s + 1) * len(GROUPS))
                        load_dense(s, t + 1)
                collect_pairs(t, first)

            tile(0, True, False)
            with sp.Fori(1, TILES - 1) as t:
                tile(t, False, False)
            tile(TILES - 1, False, True)
            stored = 0
            for a, b in ((0, TILES - 1), (TILES - 1, TILES)):
                sp.wait_ge(y_saved, b)
                for s in range(SUBS):
                    sp.dma_start(y.rearrange("(t s j i) o -> o t s j i", t=TILES, s=SUBS, j=QUADS)[:, a:b, s],
                                 y_sb[:, :].rearrange("o (t j s i) -> o t s j i", t=TILES, j=QUADS, s=SUBS)[:, a:b, s]
                                 ).then_inc(y_stored, 16)
                    stored += 16
            sp.wait_ge(y_stored, stored)

        @block.gpsimd
        def _(pool):
            pool.iota(rowid[:, :], [[1, KC]], base=0, channel_multiplier=KC,
                      allow_small_or_imprecise_dtypes=True).then_inc(consts_made, 1)
            pool.memset(ident[:, :], 0.0).then_inc(zeroed, 1)
            pool.wait_ge(zeroed, 1)
            pool.affine_select(out=ident[:, :], in_=ident[:, :], compare_op=ALU.not_equal, fill=1.0, base=0,
                               pattern=[[-1, P]], channel_multiplier=1).then_inc(consts_made, 1)
            pool.wait_ge(ids_landed, 16)

            def tile(t, first):
                for s in range(SUBS):
                    if not first:
                        pool.wait_ge(transposed, t * GT - (SUBS - 1 - s) * len(GROUPS))
                    pool.tensor_copy(ids_now[:, s, :], ids_sb[:, bass.ds(t * SUBS + s, 1), :]
                                     .rearrange("p o f -> p (o f)")).then_inc(ids_taken, 1)
                    pool.wait_ge(ids_taken, t * SUBS + s + 1)
                    pool.sem_inc(gathers_begun, 1)
                    for k, n in enumerate(GATHERED):
                        pool.indirect_dma_start(rows[:, s, 1 + k, :], None, tables[n],
                                                bass.IndirectOffsetOnAxis(ap=ids_now[:, s, k:k + 1], axis=0)
                                                ).then_inc(rows_landed[s][(1 + k) // GROUP], 16)

            tile(0, True)
            with pool.Fori(1, TILES) as t:
                tile(t, False)

        @block.tensor
        def _(pe):
            def transposes(t, s, g, first):
                a, b = GROUPS[g]
                if g == 0:
                    pe.wait_ge(dense_landed[s], t * 16 + 16)
                gathers = 16 * sum(f != DENSE for f in range(a, b))
                pe.wait_ge(rows_landed[s][g], t * gathers + gathers)
                n = s * len(GROUPS) + g
                if not (first and n < 2):
                    pe.wait_ge(transposes_saved, t * GT + (n - 1))
                for f in range(a, b):
                    mm = pe.transpose(ps_t[:, n % 2, (f - a) * P:(f - a + 1) * P], rows[:, s, f, :], ident[:, :])
                mm.then_inc(transposed, 1)

            def lookup(t, k, first):
                if first:
                    pe.wait_ge(raw_split, k + 1)
                if not (first and k < 2):
                    pe.wait_ge(lookups_saved, t * NO + max(k - 1, 0))
                for c in range(KC):
                    half, at = 2 * k + c // HALF, c % HALF
                    if at == 0:
                        pe.wait_ge(onehots_made, t * HALVES + half + 1)
                    for part, tab in enumerate((tab_hi, tab_lo)):
                        mm = pe.matmul(ps_o[:, k % 2, 0:TILE], tab[0:KR, k, c, :], onehot[0:KR, half % RING, at, :],
                                       start=(c == 0 and part == 0), stop=(c == KC - 1 and part == 1))
                    if at == HALF - 1:
                        mm.then_inc(looked_up, 1)

            def dot_products(t, s, first):
                pe.wait_ge(transposes_saved, t * GT + (s + 1) * len(GROUPS))
                pe.wait_ge(lookups_saved, t * NO + NO)
                if not (first and s == 0):
                    pe.wait_ge(gram_saved, t * SUBS + s)
                for i in range(QUAD):
                    for j in range(QUADS):
                        at = (j * QUAD + i) * F
                        mm = pe.matmul(ps_g[j * QUAD:(j + 1) * QUAD, i // BANK_I,
                                            i % BANK_I * F:(i % BANK_I + 1) * F],
                                       ct[:, s, at:at + QUAD], ct[:, s, at:at + F],
                                       start=True, stop=True, skip_group_check=True)
                mm.then_inc(gram_done, 1)

            def layer(out, chunks, ready):
                for c, (w_hi, w_lo, x_hi, x_lo) in enumerate(chunks):
                    ready(c)
                    for m, (w, x) in enumerate(((w_hi, x_hi), (w_hi, x_lo), (w_lo, x_hi))):
                        mm = pe.matmul(out, w, x, start=(c == 0 and m == 0), stop=(c == len(chunks) - 1 and m == 2))
                return mm

            def layer1(t, n, first):
                if n == 0:
                    if first:
                        pe.wait_ge(weights_split, 1)
                    else:
                        pe.wait_ge(y_saved, t)
                    pe.wait_ge(dense_split, t + 1)

                def ready(c):
                    if n == 0 and c > 0:
                        pe.wait_ge(z_split, t * ZC + c)

                cols = slice(n * P, (n + 1) * P)
                chunks = [(w1_hi[:, ZC, cols], w1_lo[:, ZC, cols], d_hi[:, :], d_lo[:, :])]
                for c, k in enumerate(ZROWS):
                    chunks.append((w1_hi[0:k, c, cols], w1_lo[0:k, c, cols], z_hi[0:k, c, :], z_lo[0:k, c, :]))
                mm = layer(ps_m[:, n // 2, n % 2, :], chunks, ready)
                if n % 2 == 1:
                    mm.then_inc(layer1_done, 1)

            def layer2(t):
                for n in range(N2):
                    def ready(c):
                        if n == 0 and c % 2 == 0:
                            pe.wait_ge(h1_split, t * (N1 // 2) + c // 2 + 1)

                    cols = slice(n * P, (n + 1) * P)
                    mm = layer(ps_m[:, 0, n, :], [(w2_hi[:, c, cols], w2_lo[:, c, cols], h1_hi[:, c, :],
                                                   h1_lo[:, c, :]) for c in range(N1)], ready)
                mm.then_inc(layer2_done, 1)

            def layer3(t):
                pe.wait_ge(h2_saved, t * N2 + N2)
                for c in range(N2):
                    mm = pe.matmul(ps_m[0:1, 1, 0, :], w3_sb[:, c:c + 1], h2[:, c, :], start=(c == 0), stop=(c == N2 - 1))
                mm.then_inc(layer3_done, 1)

            pe.wait_ge(consts_made, 2)
            for k in range(NO):
                if k >= ALONE:
                    transposes(0, 0, k - ALONE, True)
                lookup(0, k, True)
            dot_products(0, 0, True)
            for g in range(len(GROUPS)):
                transposes(0, 1, g, True)
            dot_products(0, 1, True)

            def tile(t, first_mlp, early, last):
                for k in range(NO):
                    if k >= ALONE:
                        transposes(t, 0, k - ALONE, False)
                    lookup(t, k, False)
                if not early:
                    layer3(t - 2)
                dot_products(t, 0, False)
                for g in range(len(GROUPS)):
                    transposes(t, 1, g, False)
                    if g < N1 - 1 and not last:
                        layer1(t - 1, g, first_mlp)
                if not last:
                    layer1(t - 1, N1 - 1, first_mlp)
                dot_products(t, 1, False)
                if last:
                    for n in range(N1):
                        layer1(t - 1, n, False)
                layer2(t - 1)

            pe.wait_ge(columns_landed, 16)
            tile(1, True, True, False)
            with pe.Fori(2, TILES - 1) as t:
                tile(t, False, False, False)
            tile(TILES - 1, False, False, True)
            layer3(TILES - 2)
            for n in range(N1):
                layer1(TILES - 1, n, False)
            layer2(TILES - 1)
            layer3(TILES - 1)

        @block.scalar
        def _(act):
            def save_high(k):
                act.wait_ge(raw_landed[k % 2], raw_count(k))
                act.activation(tab_hi[0:KR, k, :, :].rearrange("p c d -> p (c d)"), raw[0:KR, k % 2, :],
                               ACT.Copy).then_inc(table_highs, 1)

            def save_transposes(t, s, g, first):
                if not first and s == 0 and g == 0:
                    act.wait_ge(dense_split, t)
                a, b = GROUPS[g]
                n = s * len(GROUPS) + g
                act.wait_ge(transposed, t * GT + n + 1)
                act.activation(ct[:, s, 0:P * F].rearrange("p (b f) -> p b f", f=F)[:, :, a:b],
                               ps_t[:, n % 2, 0:(b - a) * P].rearrange("p (f b) -> p b f", b=P),
                               ACT.Copy).then_inc(transposes_saved, 1)

            def save_lookup(t, k):
                act.wait_ge(looked_up, t * HALVES + 2 * k + 2)
                act.activation(ct[:, :, 0:P * F].rearrange("p s (b f) -> p s b f", f=F)[:, :, :, SENT + k],
                               ps_o[:, k % 2, 0:TILE].rearrange("p (s b) -> p s b", s=SUBS),
                               ACT.Copy).then_inc(lookups_saved, 1)

            def save_gram(t, s, first):
                act.wait_ge(gram_done, t * SUBS + s + 1)
                if not first and s == 0:
                    act.wait_ge(scratch_written, t * 32)
                act.activation(gram[:, :, :].rearrange("p g (s c i) -> p s c i g", s=SUBS, c=2)[:, s],
                               ps_g[:, :, 0:BANK_I * F].rearrange("p c (i g) -> p c i g", g=F),
                               ACT.Copy).then_inc(gram_saved, 1)

            def save_h1(t, first):
                if first:
                    act.wait_ge(columns_landed, 16)
                else:
                    act.wait_ge(h1_split, t * (N1 // 2))
                for n in range(N1):
                    if n % 2 == 0:
                        act.wait_ge(layer1_done, t * (N1 // 2) + n // 2 + 1)
                    act.activation(h1[:, n, :], ps_m[:, n // 2, n % 2, :], ACT.Relu,
                                   bias=b1_sb[:, n:n + 1]).then_inc(h1_saved, 1)

            def save_h2(t):
                act.wait_ge(layer2_done, t + 1)
                for n in range(N2):
                    act.activation(h2[:, n, :], ps_m[:, 0, n, :], ACT.Relu,
                                   bias=b2_sb[:, n:n + 1]).then_inc(h2_saved, 1)

            def save_y(t):
                act.wait_ge(layer3_done, t + 1)
                act.activation(y_sb[:, bass.ds(t * TILE, TILE)], ps_m[0:1, 1, 0, :], ACT.Copy).then_inc(y_saved, 1)

            for k in range(NO):
                if k == 0:
                    save_high(0)
                    save_high(1)
                if k >= ALONE:
                    save_transposes(0, 0, k - ALONE, True)
                if k + 2 < NO:
                    save_high(k + 2)
                save_lookup(0, k)
            save_gram(0, 0, True)
            for g in range(len(GROUPS)):
                save_transposes(0, 1, g, True)
            save_gram(0, 1, True)

            def tile(t, first_mlp, early, last):
                for k in range(NO):
                    if k >= ALONE:
                        save_transposes(t, 0, k - ALONE, False)
                    save_lookup(t, k)
                if not early:
                    save_y(t - 2)
                save_gram(t, 0, False)
                for g in range(len(GROUPS)):
                    save_transposes(t, 1, g, False)
                if not last:
                    save_h1(t - 1, first_mlp)
                save_gram(t, 1, False)
                if last:
                    save_h1(t - 1, False)
                save_h2(t - 1)

            tile(1, True, True, False)
            with act.Fori(2, TILES - 1) as t:
                tile(t, False, False, False)
            tile(TILES - 1, False, False, True)
            save_y(TILES - 2)
            save_h1(TILES - 1, False)
            save_h2(TILES - 1)
            save_y(TILES - 1)

        @block.vector
        def _(dve):
            highs = [0]

            def split(high, low, source, waited=None):
                dve.tensor_copy(high, source).then_inc(parts_high, 1)
                highs[0] += 1
                dve.wait_ge(parts_high, highs[0] if waited is None else waited)
                return dve.tensor_tensor(low, source, high, ALU.subtract)

            def split_table(k):
                dve.wait_ge(table_highs, k + 1)
                dve.tensor_tensor(tab_lo[0:KR, k, :, :].rearrange("p c d -> p (c d)"), raw[0:KR, k % 2, :],
                                  tab_hi[0:KR, k, :, :].rearrange("p c d -> p (c d)"),
                                  ALU.subtract).then_inc(raw_split, 1)

            def onehots(t, first):
                dve.wait_ge(ids_oh_landed, t * 16 + 16)
                for k in range(NO):
                    if first:
                        split_table(k)
                    for half in (2 * k, 2 * k + 1):
                        if not (first and half < RING):
                            dve.wait_ge(looked_up, t * HALVES + (half - RING + 1))
                        shape = [P, HALF, TILE]
                        c = half % 2 * HALF
                        dve.tensor_tensor(onehot[:, half % RING, :, :],
                                          ids_oh[:, k, :].unsqueeze(1).broadcast_to(shape),
                                          rowid[:, c:c + HALF].unsqueeze(2).broadcast_to(shape),
                                          ALU.is_equal).then_inc(onehots_made, 1)

            def split_weights():
                for item, c0, nc_ in ((ITEM_W1, 0, 2), (ITEM_W1_LAST, 2, 1)):
                    dve.wait_ge(raw_landed[item % 2], raw_count(item))
                    k = ZROWS[c0]
                    split(w1_hi[0:k, c0:c0 + nc_, :].rearrange("p c n -> p (c n)"),
                          w1_lo[0:k, c0:c0 + nc_, :].rearrange("p c n -> p (c n)"),
                          raw[0:k, item % 2, 0:nc_ * HIDDEN1]).then_inc(raw_split, 1)
                item = ITEM_DENSE
                dve.wait_ge(raw_landed[item % 2], raw_count(item))
                both = h1[:, 0:2, :].rearrange("p c n -> p (c n)")
                dve.tensor_tensor(both, raw[:, item % 2, 0:HIDDEN1], raw[:, item % 2, HIDDEN1:2 * HIDDEN1],
                                  ALU.add).then_inc(raw_split, 1)
                dve.wait_ge(raw_split, item + 1)
                split(w1_hi[:, ZC, :], w1_lo[:, ZC, :], both)
                item = ITEM_W2
                dve.wait_ge(raw_landed[item % 2], raw_count(item))
                split(w2_hi[:, :, :].rearrange("p c n -> p (c n)"), w2_lo[:, :, :].rearrange("p c n -> p (c n)"),
                      raw[:, item % 2, :]).then_inc(weights_split, 1)

            def split_z(t, first):
                if not first:
                    dve.wait_ge(layer1_done, t * (N1 // 2))
                for c, k in enumerate(ZROWS):
                    dve.wait_ge(z_landed[c], t * (16 * Z_OF[c]) + 16 * Z_OF[c])
                    split(z_hi[0:k, c, :], z_lo[0:k, c, :], z[0:k, c, :],
                          t * SPLITS + (PARTS + 1 + c)).then_inc(z_split, 1)

            def split_h1(t):
                for b in range(N1 // 2):
                    dve.wait_ge(h1_saved, t * N1 + 2 * b + 2)
                    two = slice(2 * b, 2 * b + 2)
                    split(h1_hi[:, two, :], h1_lo[:, two, :], h1[:, two, :],
                          t * SPLITS + (PARTS + 1 + ZC + b)).then_inc(h1_split, 1)

            def split_dense(t, first, count):
                dve.wait_ge(transposes_saved, t * GT + (GT - len(GROUPS) + 1))
                if not first:
                    dve.wait_ge(layer1_done, t * (N1 // 2))
                view = ct[:, :, 0:P * F].rearrange("p s (j i f) -> p j s i f", j=QUADS, f=F)[:, :, :, :, DENSE]
                shape = "p (j s i) -> p j s i"
                split(d_hi[:, :].rearrange(shape, j=QUADS, s=SUBS), d_lo[:, :].rearrange(shape, j=QUADS, s=SUBS),
                      view, count).then_inc(dense_split, 1)

            dve.memset(ct[:, :, P * F:SUBW], 0.0).then_inc(parts_high, 1)
            highs[0] += 1
            dve.wait_ge(consts_made, 1)
            onehots(0, True)
            split_weights()
            split_dense(0, True, None)
            PARTS = highs[0]
            SPLITS = ZC + N1 // 2 + 1

            def tile(t, first_mlp):
                onehots(t, False)
                split_z(t - 1, first_mlp)
                split_h1(t - 1)
                split_dense(t, False, (t - 1) * SPLITS + (PARTS + SPLITS))

            tile(1, True)
            with dve.Fori(2, TILES) as t:
                tile(t, False)
            split_z(TILES - 1, False)
            split_h1(TILES - 1)


def kernel(**inputs):
    import numpy as np
    import concourse.bacc as bacc
    from concourse.bass_utils import run_bass_kernel_spmd as run

    nc = bacc.Bacc("TRN2", target_bir_lowering=False, num_devices=1)
    host = {k: np.asarray(v) for k, v in inputs.items()}
    natural = {}
    for a in range(F):
        for b in range(a + 1, F):
            natural[a, b] = len(natural)
    order = []
    for s in range(1, SHIFTS + 1):
        for p in range(F):
            a, b = ORDER[p], ORDER[(p + s) % F]
            order.append(natural[min(a, b), max(a, b)])
    w1_rows = np.array([*range(D), *(D + q for q in order), *range(D + PAIRS, 2 * D + PAIRS)])
    ids = host["ids"]
    arrays = {
        "dense": host["r_dense_features"].reshape(BATCH // P, P, D),
        "ids_rows": ids[:, GATHERED].reshape(BATCH // P, P, NG).transpose(1, 0, 2),
        "ids_flat": ids[:, ONEHOT].reshape(TILES, TILE, NO).transpose(0, 2, 1).reshape(TILES, NO * TILE),
        "w1": host["W_top1"][w1_rows],
        "w2": host["W_top2"],
        "columns": np.concatenate([host["b_top1"].reshape(N1, P), host["b_top2"].reshape(N2, P),
                                   host["W_top3"].reshape(N2, P)]).T,
    }
    arrays |= {f"tbl_{n}": host[f"tbl_{n}"] for n in range(TABLES)}
    arrays = {k: np.ascontiguousarray(a) for k, a in arrays.items()}
    arrays = {f"in_{k}": a for k, a in arrays.items()}
    aps = {k[3:]: nc.dram_tensor(k, a.shape, mybir.dt.from_np(a.dtype), kind="ExternalInput").ap()
           for k, a in arrays.items()}
    y = nc.dram_tensor("y", (BATCH, 1), F32, kind="ExternalOutput").ap()
    tables = [aps[f"tbl_{n}"] for n in range(TABLES)]
    tower(nc, aps["dense"], aps["ids_rows"], aps["ids_flat"], tables, aps["w1"], aps["w2"],
          aps["columns"], y)
    return run(nc, [arrays], core_ids=[0]).results[0]["y"]
```

```python
from concourse import mybir
import concourse.bass as bass

F32 = mybir.dt.float32
F32R = mybir.dt.float32r
I32 = mybir.dt.int32
ALU = mybir.AluOpType
ACT = mybir.ActivationFunctionType

P = 128
BATCH = 2048
D = 128
TABLES = 26
F = TABLES + 1
SUBS = 2
TILE = SUBS * P
TILES = BATCH // TILE
HIDDEN1, HIDDEN2 = 512, 256
N1 = HIDDEN1 // P

ONEHOT = [1, 4, 6, 7, 10, 11, 12, 13, 15]
GATHERED = [n for n in range(TABLES) if n not in ONEHOT]
NO, NG = len(ONEHOT), len(GATHERED)
ROWS = 1000
KC = 8
KR = ROWS // KC
UNIT = 2
PER_TABLE = KC // UNIT
UNITS = PER_TABLE * NO
RING = 9
assert UNITS % RING == 0
IDS_FIRST = 2
SPRAY = KR // 16 * 16

ORDER = [0] + [1 + n for n in GATHERED] + [1 + n for n in ONEHOT]
DENSE = 0
GROUP = 4
GROUPS = [(a, min(a + GROUP, NG)) for a in range(0, NG, GROUP)]
GT = SUBS * len(GROUPS)
ALONE = NO - len(GROUPS)

QUAD = 32
QUADS = P // QUAD
BANK_I = 16
SUBW = P * F + QUAD - F
LAYER2_AFTER = (1, 2)
PART = 8
PARTS = QUAD // PART
LAST_GROUP = len(GROUPS) - 1
assert PARTS == N1 == LAST_GROUP == 4
SHIFTS = F // 2
PAIRS = SHIFTS * F
ZC = -(-PAIRS // P)
ZROWS = [min(P, PAIRS - c * P) for c in range(ZC)]
WIDE = F + SHIFTS
BANKS_G = QUAD // BANK_I
GRAMS = SUBS * BANKS_G
RUN = SUBS * QUAD


def z_loads():
    out = []
    for s in range(1, SHIFTS + 1):
        p = 0
        while p < F:
            q = (s - 1) * F + p
            n = min(F - p, P - q % P)
            out.append((s, p, n, q // P, q % P))
            p += n
    return out


Z_LOADS = z_loads()
Z_OF = [sum(load[3] == c for load in Z_LOADS) for c in range(ZC)]


def tower(nc, dense, ids_rows, ids_flat, tables, w1, w2, b1, b2_and_w3, y):
    from contextlib import ExitStack

    ctx = ExitStack()
    with ctx:
        def sb(name, shape, dt=F32):
            return ctx.enter_context(nc.sbuf_tensor(name, shape, dt))

        def ps(name, shape):
            return ctx.enter_context(nc.psum_tensor(name, shape, F32))

        def sem(name):
            return ctx.enter_context(nc.semaphore(name))

        ident = sb("ident", [P, P])
        ids_sb = sb("ids_sb", [P, BATCH // P, NG], I32)
        ids_now = sb("ids_now", [P, SUBS, NG], I32)
        rowid = sb("rowid", [P, KC])
        ids_oh = sb("ids_oh", [P, NO, TILE], I32)
        onehot = sb("onehot", [P, RING, UNIT, TILE], F32R)
        tab_hi = sb("tab_hi", [P, NO, KC, D], F32R)
        tab_lo = sb("tab_lo", [P, NO, KC, D], F32R)
        shared = sb("shared", [P, 2 * KC * D])
        raw = shared[:, :].rearrange("p (n r) -> p n r", n=2)
        h1 = shared[:, 0:N1 * TILE].rearrange("p (n b) -> p n b", n=N1)
        z = shared[:, N1 * TILE:(N1 + ZC) * TILE].rearrange("p (c b) -> p c b", c=ZC)
        rows = sb("rows", [P, SUBS, NG, D])
        ct = sb("ct", [P, SUBS, SUBW])
        gram = sb("gram", [P, F, RUN])
        z_hi = sb("z_hi", [P, ZC, TILE], F32R)
        z_lo = sb("z_lo", [P, ZC, TILE], F32R)
        d_in = sb("d_in", [P, TILE])
        d_hi = sb("d_hi", [P, TILE], F32R)
        d_lo = sb("d_lo", [P, TILE], F32R)
        w1_hi = sb("w1_hi", [P, ZC + 1, HIDDEN1], F32R)
        w1_lo = sb("w1_lo", [P, ZC + 1, HIDDEN1], F32R)
        w2_hi = sb("w2_hi", [P, N1, HIDDEN2], F32R)
        w2_lo = sb("w2_lo", [P, N1, HIDDEN2], F32R)
        b1_sb = sb("b1_sb", [P, N1])
        b2_w3 = sb("b2_w3", [P, 2, HIDDEN2])
        h1_hi = sb("h1_hi", [P, N1, TILE], F32R)
        h1_lo = sb("h1_lo", [P, N1, TILE], F32R)
        h2 = sb("h2", [P, SUBS, HIDDEN2])
        y_sb = sb("y_sb", [P, BATCH // P])
        y_rows = sb("y_rows", [BATCH // P, P])

        ps_t = ps("ps_t", [P, 2, GROUP * P])
        ps_o = ps("ps_o", [P, 2, 512])
        ps_g = ps("ps_g", [P, 2, 512])
        ps_m = ps("ps_m", [P, 2, 2, TILE])

        ps_last = [ps_o[:, 0, 0:TILE], ps_o[:, 1, 0:TILE], ps_t[:, 0, 0:TILE], ps_t[:, 1, 0:TILE]]

        scratch = nc.dram_tensor("scratch", [P, WIDE, RUN], F32, kind="Internal")

        ids_landed = sem("ids_landed")
        raw_landed = [sem(f"raw_landed{n}") for n in range(2)]
        raw_split = sem("raw_split")
        b1_landed = sem("b1_landed")
        b2_w3_landed = sem("b2_w3_landed")
        ids_oh_first_landed = sem("ids_oh_first_landed")
        ids_oh_landed = sem("ids_oh_landed")
        dense_landed = sem("dense_landed")
        dense_placed = sem("dense_placed")
        rows_landed = [[sem(f"rows_landed{s}_{g}") for g in range(len(GROUPS))] for s in range(SUBS)]
        consts_made = sem("consts_made")
        ids_taken = sem("ids_taken")
        table_highs = sem("table_highs")
        gathers_begun = sem("gathers_begun")
        ident_zeroed = sem("ident_zeroed")
        ct_zeroed = sem("ct_zeroed")
        weight_highs = sem("weight_highs")
        z_highs = sem("z_highs")
        dense_highs = sem("dense_highs")
        h1_highs = sem("h1_highs")
        weights_split = sem("weights_split")
        onehots_made = sem("onehots_made")
        transposed = sem("transposed")
        transposes_saved = sem("transposes_saved")
        looked_up = sem("looked_up")
        lookups_saved = sem("lookups_saved")
        gram_done = sem("gram_done")
        gram_saved = sem("gram_saved")
        scratch_written = sem("scratch_written")
        z_landed = [sem(f"z_landed{c}") for c in range(ZC)]
        z_last_landed = sem("z_last_landed")
        z_split = sem("z_split")
        dense_split = sem("dense_split")
        layer1_done = sem("layer1_done")
        h1_saved = sem("h1_saved")
        h1_split = sem("h1_split")
        layer2_done = sem("layer2_done")
        h2_biased = sem("h2_biased")
        y_summed = sem("y_summed")
        y_transposed = sem("y_transposed")
        y_turned = sem("y_turned")
        y_stored = sem("y_stored")

        items = []
        for n in ONEHOT:
            table = tables[n].rearrange("(p c) d -> p (c d)", c=KC)
            items.append([(0, SPRAY, 0, KC * D, table[0:SPRAY]), (SPRAY, KR, 0, KC * D, table[SPRAY:KR])])
        w1_pairs = w1[D:D + PAIRS]
        items.append([(0, ZROWS[c], c * HIDDEN1, (c + 1) * HIDDEN1, w1_pairs[c * P:c * P + ZROWS[c]])
                      for c in (0, 1)])
        items.append([(0, ZROWS[2], 0, HIDDEN1, w1_pairs[2 * P:PAIRS])])
        items.append([(0, P, 0, HIDDEN1, w1[0:D]), (0, P, HIDDEN1, 2 * HIDDEN1, w1[D + PAIRS:2 * D + PAIRS])])
        items.append([(0, P, c * HIDDEN2, (c + 1) * HIDDEN2, w2[c * P:(c + 1) * P]) for c in range(N1)])
        ITEM_W1, ITEM_W1_LAST, ITEM_DENSE, ITEM_W2 = range(NO, NO + 4)

        def raw_count(n):
            return 16 * sum(len(items[m]) for m in range(n % 2, n + 1, 2))

        def load_pairs(eng, load, landed):
            s, p, n, c, q = load
            source = bass.AP(scratch, (p * WIDE + p + s) * RUN,
                             [[(WIDE + 1) * RUN, n], [QUAD * WIDE * RUN, QUADS], [1, RUN]])
            eng.dma_start(z[q:q + n, c, :].rearrange("p (j r) -> p j r", j=QUADS), source).then_inc(landed, 16)

        block = ctx.enter_context(nc.Block())

        @block.sync
        def _(sp):
            sp.dma_start(ids_sb[:, :, :], ids_rows).then_inc(ids_landed, 16)

            def stage(n):
                if n >= 2:
                    sp.wait_ge(raw_split, n - 1)
                for p0, p1, c0, c1, source in items[n]:
                    sp.dma_start(raw[p0:p1, n % 2, c0:c1], source).then_inc(raw_landed[n % 2], 16)

            def load_dense(t):
                sp.dma_start(d_in[:, :], dense[bass.ds(t, 1)].rearrange("o d b -> (o d) b")
                             ).then_inc(dense_landed, 16)

            def load_ids_oh(t):
                sp.dma_start(ids_oh[:, :, :].rearrange("p n b -> p (n b)"),
                             ids_flat[bass.ds(t, 1)].rearrange("o n -> (o n)")
                             .partition_broadcast(P)).then_inc(ids_oh_landed, 16)

            def collect_pairs(t, first, last):
                if first:
                    sp.wait_ge(weights_split, 1)
                else:
                    sp.wait_ge(z_split, t * ZC)
                sp.wait_ge(gram_saved, t * GRAMS + GRAMS)
                sp.dma_start(scratch[:, 0:F, :], gram[:, :, :]).then_inc(scratch_written, 16)
                sp.dma_start(scratch[:, F:WIDE, :], gram[:, 0:SHIFTS, :]).then_inc(scratch_written, 16)
                if not last:
                    sp.wait_ge(dense_split, t + 1)
                    sp.wait_ge(dense_placed, t + 1)
                    load_dense(t + 1)
                sp.wait_ge(scratch_written, t * 32 + 32)
                for load in Z_LOADS:
                    if not (last and load[3] == ZC - 1):
                        load_pairs(sp, load, z_landed[load[3]])

            for a, b, landed in ((0, IDS_FIRST, ids_oh_first_landed), (IDS_FIRST, NO, ids_oh_landed)):
                sp.dma_start(ids_oh[:, a:b, :].rearrange("p n b -> p (n b)"),
                             ids_flat[0, a * TILE:b * TILE].partition_broadcast(P)).then_inc(landed, 16)
                if a == 0:
                    stage(0)
            stage(1)
            load_dense(0)
            sp.dma_start(b1_sb[:, :], b1).then_inc(b1_landed, 16)
            sp.dma_start(b2_w3[:, :, :].rearrange("p n b -> p (n b)"), b2_and_w3.partition_broadcast(P)
                         ).then_inc(b2_w3_landed, 16)
            for n in range(2, len(items)):
                if n == NO + 2:
                    sp.wait_ge(onehots_made, UNITS)
                    load_ids_oh(1)
                stage(n)
            def tile(t, first, last):
                if not (first or last):
                    sp.wait_ge(onehots_made, t * UNITS + UNITS)
                    load_ids_oh(t + 1)
                collect_pairs(t, first, last)

            tile(0, True, False)
            with sp.Fori(1, TILES - 1) as t:
                tile(t, False, False)
            tile(TILES - 1, False, True)
            sp.wait_ge(y_turned, 1)
            sp.dma_start(y.rearrange("(s p) o -> s (p o)", p=P), y_rows[:, :]).then_inc(y_stored, 16)
            sp.wait_ge(y_stored, 16)

        @block.gpsimd
        def _(pool):
            pool.iota(rowid[:, :], [[1, KC]], base=0, channel_multiplier=KC,
                      allow_small_or_imprecise_dtypes=True).then_inc(consts_made, 1)
            pool.memset(ident[:, :], 0.0).then_inc(ident_zeroed, 1)
            pool.wait_ge(ident_zeroed, 1)
            pool.affine_select(out=ident[:, :], in_=ident[:, :], compare_op=ALU.not_equal, fill=1.0, base=0,
                               pattern=[[-1, P]], channel_multiplier=1).then_inc(consts_made, 1)
            pool.wait_ge(ids_landed, 16)

            def gathers(s, ids):
                for k, n in enumerate(GATHERED):
                    pool.indirect_dma_start(rows[:, s, k, :], None, tables[n],
                                            bass.IndirectOffsetOnAxis(ap=ids[:, s, k:k + 1], axis=0)
                                            ).then_inc(rows_landed[s][k // GROUP], 16)

            for s in range(SUBS):
                gathers(s, ids_sb)
            with pool.Fori(1, TILES) as t:
                for s in range(SUBS):
                    pool.wait_ge(ids_taken, t * SUBS - (SUBS - 1 - s))
                    pool.sem_inc(gathers_begun, 1)
                    gathers(s, ids_now)
            pool.wait_ge(z_split, (TILES - 1) * ZC)
            pool.wait_ge(scratch_written, TILES * 32)
            for load in Z_LOADS:
                if load[3] == ZC - 1:
                    load_pairs(pool, load, z_last_landed)

        @block.tensor
        def _(pe):
            def transposes(t, s, g, first):
                a, b = GROUPS[g]
                pe.wait_ge(rows_landed[s][g], t * (16 * (b - a)) + 16 * (b - a))
                n = s * len(GROUPS) + g
                if not (first and n < 2):
                    pe.wait_ge(transposes_saved, t * GT + (n - 1))
                for f in range(a, b):
                    mm = pe.transpose(ps_t[:, n % 2, (f - a) * P:(f - a + 1) * P], rows[:, s, f, :], ident[:, :])
                mm.then_inc(transposed, 1)

            def lookup(t, k, first):
                if first:
                    pe.wait_ge(raw_split, k + 1)
                if not (first and k < 2):
                    pe.wait_ge(lookups_saved, t * NO + max(k - 1, 0))
                for c in range(KC):
                    unit, at = PER_TABLE * k + c // UNIT, c % UNIT
                    if at == 0:
                        pe.wait_ge(onehots_made, t * UNITS + unit + 1)
                    for part, tab in enumerate((tab_hi, tab_lo)):
                        mm = pe.matmul(ps_o[:, k % 2, 0:TILE], tab[0:KR, k, c, :], onehot[0:KR, unit % RING, at, :],
                                       start=(c == 0 and part == 0), stop=(c == KC - 1 and part == 1))
                    if at == UNIT - 1:
                        mm.then_inc(looked_up, 1)

            def dot_products(t, s, parts, first):
                for part in parts:
                    if part == 0:
                        pe.wait_ge(transposes_saved, t * GT + (s + 1) * len(GROUPS))
                        if s == 0:
                            pe.wait_ge(dense_placed, t + 1)
                            pe.wait_ge(lookups_saved, t * NO + NO)
                    bank = part * PART // BANK_I
                    if part * PART % BANK_I == 0 and not (first and s == 0):
                        pe.wait_ge(gram_saved, t * GRAMS + ((s - 1) * BANKS_G + bank + 1))
                    for i in range(part * PART, (part + 1) * PART):
                        for j in range(QUADS):
                            at = (j * QUAD + i) * F
                            mm = pe.matmul(ps_g[j * QUAD:(j + 1) * QUAD, bank, i % BANK_I * F:(i % BANK_I + 1) * F],
                                           ct[:, s, at:at + QUAD], ct[:, s, at:at + F],
                                           start=True, stop=True, skip_group_check=True)
                    if (part + 1) * PART % BANK_I == 0:
                        mm.then_inc(gram_done, 1)

            def layer(out, chunks, ready):
                for c, (w_hi, w_lo, x_hi, x_lo) in enumerate(chunks):
                    ready(c)
                    for m, (w, x) in enumerate(((w_hi, x_hi), (w_hi, x_lo), (w_lo, x_hi))):
                        mm = pe.matmul(out, w, x, start=(c == 0 and m == 0), stop=(c == len(chunks) - 1 and m == 2))
                return mm

            def layer1(t, n, first):
                if n == 0:
                    if first:
                        pe.wait_ge(weights_split, 1)
                    else:
                        pe.wait_ge(h2_biased, t * SUBS)
                    pe.wait_ge(dense_split, t + 1)

                def ready(c):
                    if n == 0 and c > 0:
                        pe.wait_ge(z_split, t * ZC + c)

                cols = slice(n * P, (n + 1) * P)
                chunks = [(w1_hi[:, ZC, cols], w1_lo[:, ZC, cols], d_hi[:, :], d_lo[:, :])]
                for c, k in enumerate(ZROWS):
                    chunks.append((w1_hi[0:k, c, cols], w1_lo[0:k, c, cols], z_hi[0:k, c, :], z_lo[0:k, c, :]))
                mm = layer(ps_m[:, n // 2, n % 2, :], chunks, ready)
                if n % 2 == 1:
                    mm.then_inc(layer1_done, 1)

            def layer1_by_chunk(t, chunks):
                operands = [(w1_hi[:, ZC, :], w1_lo[:, ZC, :], d_hi[:, :], d_lo[:, :])]
                for c, k in enumerate(ZROWS):
                    operands.append((w1_hi[0:k, c, :], w1_lo[0:k, c, :], z_hi[0:k, c, :], z_lo[0:k, c, :]))
                for c in chunks:
                    w_hi, w_lo, x_hi, x_lo = operands[c]
                    if c == 0:
                        pe.wait_ge(dense_split, t + 1)
                    else:
                        pe.wait_ge(z_split, t * ZC + c)
                    for n in range(N1):
                        cols = slice(n * P, (n + 1) * P)
                        for m, (w, x) in enumerate(((w_hi, x_hi), (w_hi, x_lo), (w_lo, x_hi))):
                            mm = pe.matmul(ps_last[n], w[:, cols], x, start=(c == 0 and m == 0),
                                           stop=(c == ZC and m == 2), skip_group_check=True)
                        if n % 2 == 1 and c == ZC:
                            mm.then_inc(layer1_done, 1)

            def layer2(t, s):
                def ready(c):
                    if s == 0 and c % 2 == 0:
                        pe.wait_ge(h1_split, t * (N1 // 2) + c // 2 + 1)

                samples = slice(s * P, (s + 1) * P)
                layer(ps_m[:, s, 0, :], [(h1_hi[:, c, samples], h1_lo[:, c, samples], w2_hi[:, c, :],
                                          w2_lo[:, c, :]) for c in range(N1)], ready).then_inc(layer2_done, 1)

            def first_dot_products(t, first, with_layer1, first_mlp):
                for half in range(2):
                    transposes(t, 1, 2 * half, first)
                    transposes(t, 1, 2 * half + 1, first)
                    dot_products(t, 0, [2 * half], first)
                    if half == 1 and not with_layer1:
                        transposes(t, 1, LAST_GROUP, first)
                    dot_products(t, 0, [2 * half + 1], first)
                    if half == 1 and with_layer1:
                        transposes(t, 1, LAST_GROUP, first)
                    if with_layer1:
                        layer1(t - 1, half, first_mlp)

            pe.wait_ge(consts_made, 2)
            for k in range(NO):
                if k >= ALONE:
                    transposes(0, 0, k - ALONE, True)
                lookup(0, k, True)
            pe.wait_ge(ct_zeroed, 1)
            first_dot_products(0, True, False, False)
            for part in range(PARTS):
                dot_products(0, 1, [part], True)
                if part % 2 == 1:
                    lookup(1, part // 2, False)

            def tile(t, early, last):
                for k in range(2 if early else 0, NO):
                    if k >= ALONE:
                        transposes(t, 0, k - ALONE, False)
                    lookup(t, k, False)
                    if k in LAYER2_AFTER and not early:
                        layer2(t - 2, LAYER2_AFTER.index(k))
                first_dot_products(t, False, not last, early)
                for part in range(PARTS):
                    dot_products(t, 1, [part], False)
                    if part % 2 == 1 and not last:
                        layer1(t - 1, 2 + part // 2, early)
                if last:
                    for n in range(N1):
                        layer1(t - 1, n, False)
                    layer1_by_chunk(t, [0])
                    for s in range(SUBS):
                        layer2(t - 1, s)

            tile(1, True, False)
            with pe.Fori(2, TILES - 1) as t:
                tile(t, False, False)
            tile(TILES - 1, False, True)
            layer1_by_chunk(TILES - 1, range(1, ZC + 1))
            for s in range(SUBS):
                layer2(TILES - 1, s)
            pe.wait_ge(y_summed, TILES * SUBS)
            pe.transpose(ps_t[0:BATCH // P, 0, 0:P], y_sb[:, :], ident[:, :]).then_inc(y_transposed, 1)

        @block.scalar
        def _(act):
            def save_high(k):
                act.wait_ge(raw_landed[k % 2], raw_count(k))
                act.activation(tab_hi[0:KR, k, :, :].rearrange("p c d -> p (c d)"), raw[0:KR, k % 2, :],
                               ACT.Copy).then_inc(table_highs, 1)

            def save_transposes(t, s, g):
                a, b = GROUPS[g]
                n = s * len(GROUPS) + g
                act.wait_ge(transposed, t * GT + n + 1)
                act.activation(ct[:, s, 0:P * F].rearrange("p (b f) -> p b f", f=F)[:, :, 1 + a:1 + b],
                               ps_t[:, n % 2, 0:(b - a) * P].rearrange("p (f b) -> p b f", b=P),
                               ACT.Copy).then_inc(transposes_saved, 1)

            def take_ids(t, s):
                act.wait_ge(transposed, t * GT - (SUBS - 1 - s) * len(GROUPS))
                act.activation(ids_now[:, s, :], ids_sb[:, bass.ds(t * SUBS + s, 1), :]
                               .rearrange("p o f -> p (o f)"), ACT.Copy).then_inc(ids_taken, 1)

            def save_lookup(t, k):
                act.wait_ge(looked_up, t * UNITS + PER_TABLE * (k + 1))
                act.activation(ct[:, :, 0:P * F].rearrange("p s (b f) -> p s b f", f=F)[:, :, :, 1 + NG + k],
                               ps_o[:, k % 2, 0:TILE].rearrange("p (s b) -> p s b", s=SUBS),
                               ACT.Copy).then_inc(lookups_saved, 1)

            def place_dense(t):
                act.wait_ge(dense_landed, t * 16 + 16)
                act.activation(ct[:, :, 0:P * F].rearrange("p s (j i f) -> p j s i f", j=QUADS, f=F)[:, :, :, :, DENSE],
                               d_in[:, :].rearrange("p (j s i) -> p j s i", j=QUADS, s=SUBS),
                               ACT.Copy).then_inc(dense_placed, 1)

            def save_gram(t, s, bank, first):
                act.wait_ge(gram_done, t * GRAMS + s * BANKS_G + bank + 1)
                if not first and s == 0 and bank == 0:
                    act.wait_ge(scratch_written, t * 32)
                act.activation(gram[:, :, :].rearrange("p g (s c i) -> p s c i g", s=SUBS, c=BANKS_G)[:, s, bank],
                               ps_g[:, bank, 0:BANK_I * F].rearrange("p (i g) -> p i g", g=F),
                               ACT.Copy).then_inc(gram_saved, 1)

            def save_h1(t, pair, first, source=None):
                if pair == 0:
                    if first:
                        act.wait_ge(b1_landed, 16)
                    else:
                        act.wait_ge(h1_split, t * (N1 // 2))
                act.wait_ge(layer1_done, t * (N1 // 2) + pair + 1)
                for m in range(2):
                    n = 2 * pair + m
                    ps = source[n] if source else ps_m[:, pair, m, :]
                    act.activation(h1[:, n, :].rearrange("p (s j i) -> p j s i", s=SUBS, j=QUADS),
                                   ps.rearrange("p (j s i) -> p j s i", s=SUBS, j=QUADS), ACT.Relu,
                                   bias=b1_sb[:, n:n + 1]).then_inc(h1_saved, 1)

            def save_first_gram(t, first, with_layer1):
                for half in range(2):
                    save_transposes(t, 1, 2 * half)
                    save_transposes(t, 1, 2 * half + 1)
                    if half == 1 and not with_layer1:
                        save_transposes(t, 1, LAST_GROUP)
                    save_gram(t, 0, half, first)
                    if half == 1 and with_layer1:
                        save_transposes(t, 1, LAST_GROUP)

            for k in range(NO):
                if k == 0:
                    save_high(0)
                    save_high(1)
                    place_dense(0)
                if k >= ALONE:
                    save_transposes(0, 0, k - ALONE)
                if k + 2 < NO:
                    save_high(k + 2)
                save_lookup(0, k)
            act.wait_ge(ids_landed, 16)
            take_ids(1, 0)
            save_first_gram(0, True, False)
            take_ids(1, 1)
            for bank in range(BANKS_G):
                save_gram(0, 1, bank, False)

            def tile(t, first_mlp, last):
                for k in range(NO):
                    if k == ALONE:
                        place_dense(t)
                    if k >= ALONE:
                        save_transposes(t, 0, k - ALONE)
                    save_lookup(t, k)
                if not last:
                    take_ids(t + 1, 0)
                save_first_gram(t, False, not last)
                if not last:
                    take_ids(t + 1, 1)
                    save_h1(t - 1, 0, first_mlp)
                for bank in range(BANKS_G):
                    save_gram(t, 1, bank, False)
                if last:
                    save_h1(t - 1, 0, False)
                save_h1(t - 1, 1, first_mlp)

            tile(1, True, False)
            with act.Fori(2, TILES - 1) as t:
                tile(t, False, False)
            tile(TILES - 1, False, True)
            for pair in range(N1 // 2):
                save_h1(TILES - 1, pair, False, ps_last)
            act.wait_ge(y_transposed, 1)
            act.activation(y_rows[:, :], ps_t[0:BATCH // P, 0, 0:P], ACT.Copy).then_inc(y_turned, 1)

        @block.vector
        def _(dve):
            def split(high, low, source, highs, count):
                dve.tensor_copy(high, source).then_inc(highs, 1)
                dve.wait_ge(highs, count)
                return dve.tensor_tensor(low, source, high, ALU.subtract)

            def split_table(k):
                dve.wait_ge(table_highs, k + 1)
                dve.tensor_tensor(tab_lo[0:KR, k, :, :].rearrange("p c d -> p (c d)"), raw[0:KR, k % 2, :],
                                  tab_hi[0:KR, k, :, :].rearrange("p c d -> p (c d)"),
                                  ALU.subtract).then_inc(raw_split, 1)

            def output(t):
                for s in range(SUBS):
                    dve.wait_ge(layer2_done, t * SUBS + s + 1)
                    dve.tensor_tensor(h2[:, s, :], ps_m[:, s, 0, :], b2_w3[:, 0, :], ALU.add).then_inc(h2_biased, 1)
                    dve.wait_ge(h2_biased, t * SUBS + s + 1)
                    dve.scalar_tensor_tensor(h2[:, s, :], h2[:, s, :], 0.0, b2_w3[:, 1, :], ALU.max, ALU.mult,
                                             accum_out=y_sb[:, bass.ds(t * SUBS + s, 1)]).then_inc(y_summed, 1)

            def onehots(t, units, first):
                for unit in units:
                    k, c = unit // PER_TABLE, unit % PER_TABLE * UNIT
                    if not (first and unit < RING):
                        dve.wait_ge(looked_up, t * UNITS + (unit - RING + 1))
                    shape = [P, UNIT, TILE]
                    dve.tensor_tensor(onehot[:, unit % RING, :, :],
                                      ids_oh[:, k, :].unsqueeze(1).broadcast_to(shape),
                                      rowid[:, c:c + UNIT].unsqueeze(2).broadcast_to(shape),
                                      ALU.is_equal).then_inc(onehots_made, 1)

            def first_onehots(t):
                dve.wait_ge(ids_oh_landed, t * 16 + 16)
                onehots(t, range(RING), False)

            def split_pair_weights():
                for n, (c0, c1) in enumerate(((0, ZC - 1), (ZC - 1, ZC))):
                    item, k = ITEM_W1 + n, ZROWS[c0]
                    dve.wait_ge(raw_landed[item % 2], raw_count(item))
                    split(w1_hi[0:k, c0:c1, :].rearrange("p c n -> p (c n)"),
                          w1_lo[0:k, c0:c1, :].rearrange("p c n -> p (c n)"),
                          raw[0:k, item % 2, 0:(c1 - c0) * HIDDEN1], weight_highs, n + 1).then_inc(raw_split, 1)

            def split_other_weights():
                item = ITEM_DENSE
                dve.wait_ge(raw_landed[item % 2], raw_count(item))
                both = h2[:, :, :].rearrange("p c n -> p (c n)")
                dve.tensor_tensor(both, raw[:, item % 2, 0:HIDDEN1], raw[:, item % 2, HIDDEN1:2 * HIDDEN1],
                                  ALU.add).then_inc(raw_split, 1)
                dve.wait_ge(raw_split, item + 1)
                split(w1_hi[:, ZC, :], w1_lo[:, ZC, :], both, weight_highs, 3)
                item = ITEM_W2
                dve.wait_ge(raw_landed[item % 2], raw_count(item))
                split(w2_hi[:, :, :].rearrange("p c n -> p (c n)"), w2_lo[:, :, :].rearrange("p c n -> p (c n)"),
                      raw[:, item % 2, :], weight_highs, 4).then_inc(weights_split, 1)

            def split_z(t, first, last=False, chunks=range(ZC)):
                if not first and 0 in chunks:
                    dve.wait_ge(layer1_done, t * (N1 // 2))
                for c in chunks:
                    k = ZROWS[c]
                    if last and c == ZC - 1:
                        dve.wait_ge(z_last_landed, 16 * Z_OF[c])
                    else:
                        dve.wait_ge(z_landed[c], t * (16 * Z_OF[c]) + 16 * Z_OF[c])
                    split(z_hi[0:k, c, :], z_lo[0:k, c, :], z[0:k, c, :],
                          z_highs, t * ZC + c + 1).then_inc(z_split, 1)

            def split_h1(t, pair):
                dve.wait_ge(h1_saved, t * N1 + 2 * pair + 2)
                two = slice(2 * pair, 2 * pair + 2)
                split(h1_hi[:, two, :], h1_lo[:, two, :], h1[:, two, :],
                      h1_highs, t * (N1 // 2) + pair + 1).then_inc(h1_split, 1)

            def split_dense(t, first):
                dve.wait_ge(dense_landed, t * 16 + 16)
                if not first:
                    dve.wait_ge(layer1_done, t * (N1 // 2))
                split(d_hi[:, :], d_lo[:, :], d_in[:, :], dense_highs, t + 1).then_inc(dense_split, 1)

            dve.memset(ct[:, :, P * F:SUBW], 0.0).then_inc(ct_zeroed, 1)
            dve.wait_ge(consts_made, 1)
            dve.wait_ge(ids_oh_first_landed, 16)
            onehots(0, range(IDS_FIRST * PER_TABLE), True)
            for k in range(NO):
                split_table(k)
                if k == 0:
                    dve.wait_ge(ids_oh_landed, 16)
                    onehots(0, range(IDS_FIRST * PER_TABLE, RING), True)
                else:
                    onehots(0, range(RING + (k - 1) * PER_TABLE, min(RING + k * PER_TABLE, UNITS)), True)
            split_pair_weights()
            first_onehots(1)
            split_other_weights()
            split_dense(0, True)

            def tile(t, early, last):
                onehots(t, range(RING, UNITS), False)
                if not early:
                    output(t - 2)
                split_z(t - 1, early)
                if not last:
                    first_onehots(t + 1)
                split_h1(t - 1, 0)
                split_dense(t, False)
                split_h1(t - 1, 1)

            dve.wait_ge(b2_w3_landed, 16)
            tile(1, True, False)
            with dve.Fori(2, TILES - 1) as t:
                tile(t, False, False)
            tile(TILES - 1, False, True)
            split_z(TILES - 1, False, True, [0])
            output(TILES - 2)
            split_z(TILES - 1, False, True, range(1, ZC))
            for pair in range(N1 // 2):
                split_h1(TILES - 1, pair)
            output(TILES - 1)


def kernel(**inputs):
    import numpy as np
    import concourse.bacc as bacc
    from concourse.bass_utils import run_bass_kernel_spmd as run

    nc = bacc.Bacc("TRN2", target_bir_lowering=False, num_devices=1)
    host = {k: np.asarray(v) for k, v in inputs.items()}
    natural = {}
    for a in range(F):
        for b in range(a + 1, F):
            natural[a, b] = len(natural)
    order = []
    for s in range(1, SHIFTS + 1):
        for p in range(F):
            a, b = ORDER[p], ORDER[(p + s) % F]
            order.append(natural[min(a, b), max(a, b)])
    w1_rows = np.array([*range(D), *(D + q for q in order), *range(D + PAIRS, 2 * D + PAIRS)])
    ids = host["ids"]
    arrays = {
        "dense": host["r_dense_features"].reshape(TILES, SUBS, QUADS, QUAD, D).transpose(0, 4, 2, 1, 3)
        .reshape(TILES, D, TILE),
        "ids_rows": ids[:, GATHERED].reshape(BATCH // P, P, NG).transpose(1, 0, 2),
        "ids_flat": ids[:, ONEHOT].reshape(TILES, TILE, NO).transpose(0, 2, 1).reshape(TILES, NO * TILE),
        "w1": host["W_top1"][w1_rows],
        "w2": host["W_top2"],
        "b1": host["b_top1"].reshape(N1, P).T,
        "b2_and_w3": np.concatenate([host["b_top2"], host["W_top3"][:, 0]]),
    }
    arrays |= {f"tbl_{n}": host[f"tbl_{n}"] for n in range(TABLES)}
    arrays = {k: np.ascontiguousarray(a) for k, a in arrays.items()}
    arrays = {f"in_{k}": a for k, a in arrays.items()}
    aps = {k[3:]: nc.dram_tensor(k, a.shape, mybir.dt.from_np(a.dtype), kind="ExternalInput").ap()
           for k, a in arrays.items()}
    y = nc.dram_tensor("y", (BATCH, 1), F32, kind="ExternalOutput").ap()
    tables = [aps[f"tbl_{n}"] for n in range(TABLES)]
    tower(nc, aps["dense"], aps["ids_rows"], aps["ids_flat"], tables, aps["w1"], aps["w2"],
          aps["b1"], aps["b2_and_w3"], y)
    return run(nc, [arrays], core_ids=[0]).results[0]["y"]
```
